# Optimizing a Trainium2 kernel written in Bass

```python
import numpy as np
import jax
import jax.numpy as jnp

def _softmax(x, axis=-1):
    return jax.nn.softmax(x, axis=axis)

def _gelu(x):
    return jax.nn.gelu(x, approximate=True)

def _silu(x):
    return jax.nn.silu(x)

def _sigmoid(x):
    return jax.nn.sigmoid(x)

def _layernorm(x, axis=-1, eps=1e-05):
    m = jnp.mean(x, axis=axis, keepdims=True)
    v = jnp.var(x, axis=axis, keepdims=True)
    return (x - m) / jnp.sqrt(v + eps)

def _scatter_add(tgt, idx, src, axis=0):
    return tgt.at[idx].add(src)

def _segment_sum(src, seg, n):
    return jax.ops.segment_sum(src, seg, n)
kernel_name = 'mk_metaformer_d1_conv_nchw384_r4_7182b7'

def setup_inputs(seed: int=0):
    np.random.seed(seed)
    _w = jnp.asarray

    def _rec_inputs():
        import jax
        import jax.numpy as jnp
        _gk = jax.random.key(seed)
        x = -0.0001476 + 0.9999 * jax.random.normal(jax.random.fold_in(_gk, 1), (32, 96, 56, 56), jnp.float32)
        return x
    x = _rec_inputs()

    def _L0_conv_setup():
        import jax, jax.numpy as jnp
        import numpy as np
        HEADS = 8
        HEAD_DIM = 48
        FOLD = 2
        PROP = 4
        EPS = 1e-12

        def _fold(t, f):
            b, c, Wd, Hd = t.shape
            w, h = (Wd // f, Hd // f)
            t = t.reshape(b, c, f, w, f, h).transpose(0, 2, 4, 1, 3, 5)
            return t.reshape(b * f * f, c, w, h)

        def _unfold(t, f):
            bff, c, w, h = t.shape
            b = bff // (f * f)
            t = t.reshape(b, f, f, c, w, h).transpose(0, 3, 1, 4, 2, 5)
            return t.reshape(b, c, f * w, f * h)

        def _adaptive_avg_pool(t, pw, ph):
            b, c, w, h = t.shape
            return t.reshape(b, c, pw, w // pw, ph, h // ph).mean(axis=(3, 5))
        key = jax.random.key(seed)
        ks = jax.random.split(key, 6)
        B, C, H, W = (32, 96, 56, 56)
        D = HEADS * HEAD_DIM
        return {'x': jax.random.normal(ks[0], (B, C, H, W), jnp.float32), 'Wf': jax.random.normal(ks[1], (D, C), jnp.float32) * 0.02, 'bf': jnp.zeros((D,), jnp.float32), 'Wv': jax.random.normal(ks[2], (D, C), jnp.float32) * 0.02, 'bv': jnp.zeros((D,), jnp.float32), 'Wp': jax.random.normal(ks[3], (C, D), jnp.float32) * 0.02, 'bp': jnp.zeros((C,), jnp.float32), 'sim_alpha': jnp.ones((1,), jnp.float32), 'sim_beta': jnp.zeros((1,), jnp.float32)}
    _L0_conv_all = _L0_conv_setup()
    _L0_conv_in = {k: v for k, v in _L0_conv_all.items() if k in ('Wf', 'bf', 'Wv', 'bv', 'Wp', 'bp', 'sim_alpha', 'sim_beta')}
    del _L0_conv_all

    def _L0_ffn_setup():
        import jax, jax.numpy as jnp
        import numpy as np
        NUM_GROUPS = 5
        EPS = 1e-05
        QB = 128.0

        def _binarize_weights_groupwise(W):
            n_out = W.shape[0]
            gs = n_out // NUM_GROUPS
            Wb = jnp.zeros_like(W)
            for g in range(NUM_GROUPS):
                wg = W[g * gs:(g + 1) * gs]
                z = wg - wg.mean()
                ste = z + jax.lax.stop_gradient(jnp.sign(z) - z)
                Wb = Wb.at[g * gs:(g + 1) * gs].set(ste)
            return Wb

        def _quantize_activations_groupwise(x):
            n = x.shape[0]
            gs = n // NUM_GROUPS
            xq = jnp.zeros_like(x)
            for g in range(NUM_GROUPS):
                ag = x[g * gs:(g + 1) * gs]
                gamma = jnp.max(jnp.abs(ag))
                xq = xq.at[g * gs:(g + 1) * gs].set(jnp.clip(ag * QB / (gamma + EPS), -QB + EPS, QB - EPS))
            return xq

        def _bitlinear(x, W, b):
            Wb = _binarize_weights_groupwise(W)
            y = jnp.einsum('btc,oc->bto', x, Wb) + b
            return _quantize_activations_groupwise(y)
        key = jax.random.key(seed)
        k1, k2, k3, k4, k5 = jax.random.split(key, 5)
        B, T, C = (10, 512, 96)
        H = 4 * C
        lim1 = 1.0 / np.sqrt(C)
        lim2 = 1.0 / np.sqrt(H)
        x = jax.random.normal(k1, (B, T, C), dtype=jnp.float32)
        W1 = jax.random.uniform(k2, (H, C), minval=-lim1, maxval=lim1, dtype=jnp.float32)
        b1 = jax.random.uniform(k3, (H,), minval=-lim1, maxval=lim1, dtype=jnp.float32)
        W2 = jax.random.uniform(k4, (C, H), minval=-lim2, maxval=lim2, dtype=jnp.float32)
        b2 = jax.random.uniform(k5, (C,), minval=-lim2, maxval=lim2, dtype=jnp.float32)
        return {'x': x, 'W1': W1, 'b1': b1, 'W2': W2, 'b2': b2}
    _L0_ffn_all = _L0_ffn_setup()
    _L0_ffn_in = {k: v for k, v in _L0_ffn_all.items() if k in ('W1', 'b1', 'W2', 'b2')}
    del _L0_ffn_all
    return {'x': x, 'L0_conv_Wf': _L0_conv_in['Wf'], 'L0_conv_bf': _L0_conv_in['bf'], 'L0_conv_Wv': _L0_conv_in['Wv'], 'L0_conv_bv': _L0_conv_in['bv'], 'L0_conv_Wp': _L0_conv_in['Wp'], 'L0_conv_bp': _L0_conv_in['bp'], 'L0_conv_sim_alpha': _L0_conv_in['sim_alpha'], 'L0_conv_sim_beta': _L0_conv_in['sim_beta'], 'L0_ffn_W1': _L0_ffn_in['W1'], 'L0_ffn_b1': _L0_ffn_in['b1'], 'L0_ffn_W2': _L0_ffn_in['W2'], 'L0_ffn_b2': _L0_ffn_in['b2']}

def reference(x, L0_conv_Wf, L0_conv_bf, L0_conv_Wv, L0_conv_bv, L0_conv_Wp, L0_conv_bp, L0_conv_sim_alpha, L0_conv_sim_beta, L0_ffn_W1, L0_ffn_b1, L0_ffn_W2, L0_ffn_b2):
    import jax
    import jax.numpy as jnp

    def _L0_conv_ref(x, Wf, bf, Wv, bv, Wp, bp, sim_alpha, sim_beta):
        import jax, jax.numpy as jnp
        import numpy as np
        HEADS = 8
        HEAD_DIM = 48
        FOLD = 2
        PROP = 4
        EPS = 1e-12

        def _fold(t, f):
            b, c, Wd, Hd = t.shape
            w, h = (Wd // f, Hd // f)
            t = t.reshape(b, c, f, w, f, h).transpose(0, 2, 4, 1, 3, 5)
            return t.reshape(b * f * f, c, w, h)

        def _unfold(t, f):
            bff, c, w, h = t.shape
            b = bff // (f * f)
            t = t.reshape(b, f, f, c, w, h).transpose(0, 3, 1, 4, 2, 5)
            return t.reshape(b, c, f * w, f * h)

        def _adaptive_avg_pool(t, pw, ph):
            b, c, w, h = t.shape
            return t.reshape(b, c, pw, w // pw, ph, h // ph).mean(axis=(3, 5))
        v = jnp.einsum('bchw,dc->bdhw', x, Wv) + bv[None, :, None, None]
        f = jnp.einsum('bchw,dc->bdhw', x, Wf) + bf[None, :, None, None]

        def split_heads(t):
            b, d, w, h = t.shape
            return t.reshape(b * HEADS, d // HEADS, w, h)
        f = _fold(split_heads(f), FOLD)
        v = _fold(split_heads(v), FOLD)
        b, c, w, h = f.shape
        centers = _adaptive_avg_pool(f, PROP, PROP)
        vc = _adaptive_avg_pool(v, PROP, PROP).reshape(b, c, -1).transpose(0, 2, 1)
        cen = centers.reshape(b, c, -1).transpose(0, 2, 1)
        tok = f.reshape(b, c, -1).transpose(0, 2, 1)
        cen_n = cen / jnp.maximum(jnp.linalg.norm(cen, axis=-1, keepdims=True), EPS)
        tok_n = tok / jnp.maximum(jnp.linalg.norm(tok, axis=-1, keepdims=True), EPS)
        sim = jax.nn.sigmoid(sim_beta + sim_alpha * jnp.einsum('bmc,bnc->bmn', cen_n, tok_n))
        idx = jnp.argmax(sim, axis=1)
        mask = jax.nn.one_hot(idx, sim.shape[1], dtype=sim.dtype).transpose(0, 2, 1)
        sim = sim * mask
        v2 = v.reshape(b, c, -1).transpose(0, 2, 1)
        agg = (jnp.einsum('bmn,bnc->bmc', sim, v2) + vc) / (sim.sum(-1, keepdims=True) + 1.0)
        out = jnp.einsum('bmn,bmc->bnc', sim, agg)
        out = out.transpose(0, 2, 1).reshape(b, c, w, h)
        out = _unfold(out, FOLD)
        be, _, W2, H2 = out.shape
        out = out.reshape(be // HEADS, HEADS * c, W2, H2)
        out = jnp.einsum('bdhw,od->bohw', out, Wp) + bp[None, :, None, None]
        return out

    def _L0_ffn_ref(x, W1, b1, W2, b2):
        import jax, jax.numpy as jnp
        import numpy as np
        NUM_GROUPS = 5
        EPS = 1e-05
        QB = 128.0

        def _binarize_weights_groupwise(W):
            n_out = W.shape[0]
            gs = n_out // NUM_GROUPS
            Wb = jnp.zeros_like(W)
            for g in range(NUM_GROUPS):
                wg = W[g * gs:(g + 1) * gs]
                z = wg - wg.mean()
                ste = z + jax.lax.stop_gradient(jnp.sign(z) - z)
                Wb = Wb.at[g * gs:(g + 1) * gs].set(ste)
            return Wb

        def _quantize_activations_groupwise(x):
            n = x.shape[0]
            gs = n // NUM_GROUPS
            xq = jnp.zeros_like(x)
            for g in range(NUM_GROUPS):
                ag = x[g * gs:(g + 1) * gs]
                gamma = jnp.max(jnp.abs(ag))
                xq = xq.at[g * gs:(g + 1) * gs].set(jnp.clip(ag * QB / (gamma + EPS), -QB + EPS, QB - EPS))
            return xq

        def _bitlinear(x, W, b):
            Wb = _binarize_weights_groupwise(W)
            y = jnp.einsum('btc,oc->bto', x, Wb) + b
            return _quantize_activations_groupwise(y)
        h = _bitlinear(x, W1, b1)
        h = jax.nn.gelu(h, approximate=False)
        out = _bitlinear(h, W2, b2)
        return out

    def _gn(v, G=32, eps=1e-05):
        B_, C_, H_, W_ = v.shape
        g = v.reshape(B_, G, C_ // G, H_, W_)
        m = jnp.mean(g, axis=(2, 3, 4), keepdims=True)
        s = jnp.var(g, axis=(2, 3, 4), keepdims=True)
        return ((g - m) / jnp.sqrt(s + eps)).reshape(v.shape)

    def _ln_c(v, eps=1e-06):
        m = jnp.mean(v, axis=1, keepdims=True)
        s = jnp.var(v, axis=1, keepdims=True)
        return (v - m) / jnp.sqrt(s + eps)

    def _ln_t(v, eps=1e-05):
        m = jnp.mean(v, axis=-1, keepdims=True)
        s = jnp.var(v, axis=-1, keepdims=True)
        return (v - m) / jnp.sqrt(s + eps)

    def _to_tokens(v):
        B_, C_, H_, W_ = v.shape
        return v.reshape(B_, C_, H_ * W_).transpose(0, 2, 1)

    def _from_tokens(t, like):
        B_, C_, H_, W_ = like.shape
        return t.transpose(0, 2, 1).reshape(B_, C_, H_, W_)
    x = x + _L0_conv_ref(_ln_c(x), L0_conv_Wf, L0_conv_bf, L0_conv_Wv, L0_conv_bv, L0_conv_Wp, L0_conv_bp, L0_conv_sim_alpha, L0_conv_sim_beta)
    t = _to_tokens(x)
    t = t + _L0_ffn_ref(_ln_t(t), L0_ffn_W1, L0_ffn_b1, L0_ffn_W2, L0_ffn_b2)
    x = _from_tokens(t, x)
    return x

_drawn_inputs = setup_inputs


def setup_inputs(seed=0):
    import zlib

    import numpy as np

    out = dict(_drawn_inputs(seed))
    spreads = {'L0_conv_bf': (0.0, 0.8), 'L0_conv_bv': (0.0, 0.328), 'L0_conv_bp': (0.0, 0.1)}
    factors = {'L0_conv_Wf': 5.204, 'L0_conv_Wv': 4.999, 'L0_ffn_b1': 8.0, 'L0_ffn_b2': 8.0}
    for name, (base, spread) in spreads.items():
        noise = np.random.default_rng([zlib.crc32(name.encode()), seed]).standard_normal(out[name].shape)
        drawn = base * np.exp(spread * noise) if base else spread * noise
        out[name] = jnp.asarray(drawn.astype(out[name].dtype))
    for name, factor in factors.items():
        out[name] = (out[name] * factor).astype(out[name].dtype)
    return out
```

```python
import numpy as np
import concourse.bass as bass
from concourse import mybir
from contextlib import ExitStack

IMAGES, C, SIDE = 32, 96, 56
PIX = SIDE * SIDE
QS = SIDE // 2
QN = QS * QS
HEADS, HD, CENTERS = 8, 48, 16
D = HEADS * HD
HM = HEADS * CENTERS
ROWS_T = 4
T = QS // ROWS_T
TN = ROWS_T * QS
PW = QS // 4
HALF = PIX // 2
TA = 4
NA, NB = TA * TN, (T - TA) * TN
GROUPS, GSIZE = 5, IMAGES // 5
GQ = GSIZE * 4
XB = 4
BODY = 2 * XB
BODIES = GQ // BODY
F = 4 * C
FC = F // 128
G1, G2 = F // GROUPS, C // GROUPS
HT = QN // 2
VN = 2 * C + 2
EPS_C, EPS_T, EPS_Q, QB = 1e-6, 1e-5, 1e-5, 128.0
QCLIP = float(np.float32(QB - EPS_Q))
NORM_FLOOR = 1e-24
START = 16
LOADS = 14
POOL_SETS = 6
DVE_SUMS, DVE_SIGNS, DVE_ALL = 4, 20, 24
CONSTS = {}


def shape_constants():
    parts = {"ident": np.eye(128), "ones": np.ones((128, 128))}
    j, m = np.meshgrid(np.arange(HM), np.arange(HM), indexing="ij")
    same = j // CENTERS == m // CENTERS
    parts["first"] = np.where(same & (j < m), 1.0, 0.0) - np.eye(HM)
    pool = np.zeros((128, T, CENTERS))
    for t in range(T):
        for p in range(TN):
            row, col = ROWS_T * t + p // QS, p % QS
            pool[p, t, row // PW * 4 + col // PW] = 1.0
    parts["pool"] = pool.reshape(128, -1)
    p = np.arange(128)
    parts["head_of_row"] = np.stack([p < HD, (p >= HD) & (p < 2 * HD)], 1)
    parts["head_of_center"] = np.stack([p // CENTERS % 2 == 0, p // CENTERS % 2 == 1], 1)
    parts["bias_part"] = np.stack([p == C, p == C + 1], 1)
    parts["last_row"] = np.stack([p == C, p == C], 1)
    at = 0
    for name, a in parts.items():
        CONSTS[name] = (at, a.shape[1])
        at += a.shape[1]
    return np.concatenate([a.astype(np.float32) for a in parts.values()], 1)


SHAPE_CONSTANTS = shape_constants()


def build(nc, x, Wf, bf, Wv, bv, Wp, bp, alpha, beta, W1, b1, W2, b2, consts, out):
    f32, f16, bf16 = mybir.dt.float32, mybir.dt.float16, mybir.dt.bfloat16
    ALU, ACT, AX = mybir.AluOpType, mybir.ActivationFunctionType, mybir.AxisListType
    MAX = bass.bass_isa.ReduceOp.max
    ctx = ExitStack()
    with ctx:
        def sb(name, shape, dt=f32):
            return ctx.enter_context(nc.sbuf_tensor(name, shape, dt))

        def sem(name):
            return ctx.enter_context(nc.semaphore(name))

        ps = ctx.enter_context(nc.psum_tensor("ps", [128, 8, 512], f32))

        xbuf = sb("xbuf", [C, XB, HALF])
        tok = sb("tok", [C + 2, GQ, 2, QN], f16)
        xq = sb("xq", [C, 2, QN])
        tq = sb("tq", [C, 2, QN])
        xnT = sb("xnT", [TN, 4, T, C + 1])
        xn = sb("xn", [C + 1, 2, QN])
        cenx = sb("cenx", [C + 1, 4, CENTERS])
        cbd = sb("cbd", [C, 2, 4, 2, CENTERS])
        csq = sb("csq", [C, 2, HM])
        cn2 = sb("cn2", [C + 1, 2, HM])
        cinv = sb("cinv", [C + 1, 2, HM])
        Q = sb("Q", [C + 1, 2, HM])
        sq = sb("sq", [TN, T, D])
        n2 = sb("n2", [TN, 2, T * HEADS])
        n2c = sb("n2c", [TN, 2, T * HEADS])
        ninv = sb("ninv", [TN, 2, T * HEADS])
        cosb = sb("cosb", [TN, T * HM])
        sig = sb("sig", [TN, 2, T * HM])
        top = sb("top", [TN, T * HEADS])
        eq = sb("eq", [TN, T * HM], bf16)
        eqT = sb("eqT", [HM, QN], bf16)
        sim = sb("sim", [TN, 2, T * HM])
        simT = sb("simT", [HM, QN])
        uT = sb("uT", [C + 1, HM])
        rden = sb("rden", [HM, 1])
        hmul = sb("hmul", [HM, 2])
        a1 = sb("a1", [HM, C])
        aggp = sb("aggp", [HM, C])
        nT = sb("nT", [TN, 2, T, C + 2])
        st = {s: sb(f"st_{s}", [TN, 2, T, 6]) for s in "xt"}
        mo = {s: sb(f"mo_{s}", [TN, 2, 9, T]) for s in "xt"}
        hmax = sb("hmax", [128, GQ * 2 * FC])
        ymax = sb("ymax", [C, GQ * 2])
        gam = sb("gam", [128, 2, 2])
        den = sb("den", [128, 2, 2])
        scale = sb("scale", [128, 2])
        gel = sb("gel", [128, 2, FC * HT])
        ghi = sb("ghi", [128, 2, FC * HT], f16)
        glo = sb("glo", [128, 2, FC * HT], f16)
        cst = sb("cst", [128, SHAPE_CONSTANTS.shape[1]])
        ident16 = sb("ident16", [128, 128], bf16)
        first16 = sb("first16", [HM, HM], bf16)
        halfpow = sb("halfpow", [128, HM])
        wf = sb("wf", [C, 4, C + 1])
        wfT = sb("wfT", [C + 1, D])
        V = sb("V", [C + 1, 4, VN])
        b1h = sb("b1h", [C + 2, F], f16)
        wsum1, wsum2 = sb("wsum1", [G1, GROUPS]), sb("wsum2", [G2, GROUPS])
        wmean1, wmean2 = sb("wmean1", [G1, GROUPS]), sb("wmean2", [G2, GROUPS])
        w1T = sb("w1T", [C + 2, F], f16)
        w2T = sb("w2T", [128, FC, C], f16)
        b2c, bpc = sb("b2c", [C, 1]), sb("bpc", [C, 1])
        alphac, betac = sb("alphac", [C + 1, 1]), sb("betac", [TN, 1])

        def const(name, rows=128):
            at, n = CONSTS[name]
            return cst[0:rows, at:at + n]

        def bank(b, rows, n, at=0):
            return ps[0:rows, b, at:at + n]

        def pair(b, rows, n):
            return ps[0:rows, b:b + 2, :].rearrange("p b n -> p (b n)")[:, 0:n]

        ident, ones = const("ident"), const("ones")
        poolm = const("pool", TN).rearrange("p (t m) -> p t m", t=T)
        y32 = tok[:, :, :, :].rearrange("p q s n -> p (q s n)").bitcast(f32).rearrange("p (q n) -> p q n", n=QN)

        room = [0]

        def early(rows, *shape):
            n = int(np.prod(shape))
            a = y32.rearrange("p q n -> p (q n)")[0:rows, room[0]:room[0] + n]
            room[0] += n
            names = "abc"[:len(shape)]
            return a.rearrange(f"p ({' '.join(names)}) -> p {' '.join(names)}", **dict(zip(names, shape)))

        wv, wp = early(C, 4, C + 1), early(C, D)
        wph = early(C, 4, 2, C)
        w1, gt1, w2, gt2 = early(G1, GROUPS, C), early(G1, GROUPS, C), early(G2, GROUPS, F), early(G2, GROUPS, F)
        b1s, b1l = early(C + 2, F), early(C + 2, F)

        NAMES = """x_side x_T x_stats x_sum x_dif x_m2 x_half x_d2 x_v x_var x_rstd x_norm xn_ps xn_copied cen_x cen_f cen_bd
            cen_sq q_ps cen_n2 cen_inv q_done s_ps n2_done n2_floor n_inv cos_done sig_done top_done eq_done
            eqT_ps eqT_copied first_ps sim_done simT_ps simT_copied u_ps u_done a_ps a_rden a_mul a_half a_done o_ps t_done t_placed
            t_T t_stats t_sum t_dif t_m2 t_half t_d2 t_v t_var t_rstd t_norm n_ps n_hi n_lo c_min c_max""".split()
        S = {n: sem("s_" + n) for n in NAMES}
        f_ps, f_sq = sem("f_ps"), sem("f_sq")
        h_ps, h_max = sem("h_ps"), sem("h_max")
        bh_ps, b_gelu, b_hi, b_lo, by_ps, b_y, b_ymax = (
            sem(n) for n in ("bh_ps", "b_gelu", "b_hi", "b_lo", "by_ps", "b_y", "b_ymax"))
        STARTED = list(S.values()) + [f_ps, f_sq, h_ps, h_max, bh_ps, b_gelu, b_hi, b_lo, by_ps, b_y, b_ymax]
        x_in = [sem(f"x_in{j}") for j in range(XB)]
        t_out = [sem(f"t_out{j}") for j in range(XB)]
        waited = sem("waited")
        c_half = sem("c_half")
        g_max, g_all, g_eps, g_rec, g_scale = (sem(n) for n in ("g_max", "g_all", "g_eps", "g_rec", "g_scale"))
        w_loaded, pe_set, dve_set, pool_set = sem("w_loaded"), sem("pe_set"), sem("dve_set"), sem("pool_set")

        def done(eng, name, q):
            eng.wait_ge(S[name], q + (START + 1))

        def pipeline(eng, g, steps, bodies):
            def slots(js, first, use, filled, tail):
                for j in js:
                    for lag, step in steps:
                        d = j - lag
                        if (d >= 0 or filled) and not (tail and d >= BODY):
                            step(d % BODY, g * GQ + first + d, first + d, use, tail and d == BODY - 1)
            use = g * (2 * BODIES)
            slots(range(BODY), 0, use, False, False)
            if bodies > 1:
                with eng.Fori(1, bodies) as b:
                    slots(range(BODY), b * BODY, use + b, True, False)
            slots(range(BODY, BODY + max(lag for lag, _ in steps)), (bodies - 1) * BODY, use, True, True)

        def image_rows(k, lo=0, n=QS):
            v = xbuf[:, k // 2, :].rearrange("c (r w) -> c r w", w=SIDE)
            return v[:, lo:lo + n, k % 2 * QS:(k % 2 + 1) * QS]

        block = ctx.enter_context(nc.Block())

        @block.sync
        def _(sp):
            for s in STARTED:
                sp.sem_inc(s, START)
            per_row = [(cst[:, :], consts), (w1[:, :, :], W1[0:G1 * GROUPS, :].rearrange("(g r) c -> r g c", g=GROUPS)),
                       (w2[:, :, :], W2[0:G2 * GROUPS, :].rearrange("(g r) f -> r g f", g=GROUPS)),
                       (wf[:, :, 0:C], Wf.rearrange("(k r) c -> r k c", k=4)),
                       (wv[:, :, 0:C], Wv.rearrange("(k r) c -> r k c", k=4)),
                       (wf[:, :, C:C + 1], bf.rearrange("(k r a) -> r k a", k=4, a=1)),
                       (wv[:, :, C:C + 1], bv.rearrange("(k r a) -> r k a", k=4, a=1)),
                       (wp[:, :], Wp),
                       (b1s[C:C + 1, :], b1.rearrange("(a f) -> a f", a=1)),
                       (b1s[C + 1:C + 2, :], b1.rearrange("(a f) -> a f", a=1)),
                       (b2c[:, :], b2.rearrange("(c a) -> c a", a=1)), (bpc[:, :], bp.rearrange("(c a) -> c a", a=1)),
                       (alphac[:, :], alpha.rearrange("(c a) -> c a", a=1).broadcast_to([C + 1, 1])),
                       (betac[:, :], beta.rearrange("(c a) -> c a", a=1).broadcast_to([TN, 1]))]
            assert len(per_row) == LOADS
            with nc.allow_non_contiguous_dma(reason="a bias as a column: a few hundred numbers"):
                for dst, src in per_row:
                    sp.dma_start(dst, src).then_inc(w_loaded, 16)

            x_half = x.rearrange("i c (s h) w -> i s c (h w)", s=2)
            o_half = out.rearrange("i c (s h) w -> i s c (h w)", s=2)

            def half(a, image, j):
                return a[bass.ds(image + j // 2, 1), j % 2, :, :].rearrange("a c n -> c (a n)")

            def load(src, image, j):
                sp.dma_start(xbuf[:, j, :], half(src, image, j)).then_inc(x_in[j], 16)

            def store(image, j):
                sp.dma_start(half(o_half, image, j), xbuf[:, j, :]).then_inc(t_out[j], 16)

            def attention(g, bodies):
                def body(b, last):
                    for j in range(XB):
                        image = g * GSIZE + b * (XB // 2)
                        done(sp, "t_placed", g * GQ + b * BODY + (2 * j + 1))
                        store(image, j)
                        sp.wait_ge(t_out[j], (g * (2 * BODIES) + b) * 16 + 16)
                        sp.sem_inc(waited, 1)
                        if not last:
                            load(x_half, image + XB // 2, j)
                for j in range(XB):
                    load(x_half, g * GSIZE, j)
                if bodies > 1:
                    with sp.Fori(0, bodies - 1) as b:
                        body(b, False)
                body(bodies - 1, True)

            with sp.Fori(0, GROUPS) as g:
                attention(g, BODIES)
                for j in range(XB):
                    load(o_half, g * GSIZE, j)

                def finish(b, last):
                    for j in range(XB):
                        sp.wait_ge(c_half, g * (2 * GSIZE) + b * XB + (j + 1))
                        store(g * GSIZE + b * (XB // 2), j)
                        sp.wait_ge(t_out[j], (g * (2 * BODIES) + b) * 16 + (BODIES + 1) * 16)
                        sp.sem_inc(waited, 1)
                        if not last:
                            load(o_half, g * GSIZE + (b + 1) * (XB // 2), j)
                with sp.Fori(0, BODIES - 1) as b:
                    finish(b, False)
                finish(BODIES - 1, True)
            attention(GROUPS, 1)

        @block.gpsimd
        def _(pool):
            nc.gpsimd.memset(halfpow[:, :], -0.5).then_inc(pool_set, 1)
            nc.gpsimd.memset(xnT[:, :, :, C:C + 1], 1.0).then_inc(pool_set, 1)
            nc.gpsimd.memset(nT[:, :, :, C:C + 2], 1.0).then_inc(pool_set, 1)
            nc.gpsimd.memset(w1T[:, :], 0.0).then_inc(pool_set, 1)
            nc.gpsimd.memset(w2T[:, :, :], 0.0).then_inc(pool_set, 1)
            nc.gpsimd.memset(gam[:, :, :], 0.0).then_inc(pool_set, 1)
            pool.wait_ge(pool_set, POOL_SETS)

            def met():
                pool.sem_inc(waited, 1)

            def moments(s, eps):
                def step(k, q, place, use, last):
                    b = k % 2
                    a, w = st[s][:, b, :, :], mo[s][:, b, :, :]
                    done(pool, s + "_stats", q)
                    done(pool, s + "_norm", q - 2)
                    nc.gpsimd.tensor_tensor(w[:, 0, :], a[:, :, 1], a[:, :, 4], ALU.add).then_inc(S[s + "_sum"], 1)
                    nc.gpsimd.tensor_tensor(w[:, 1, :], a[:, :, 1], a[:, :, 4], ALU.subtract).then_inc(S[s + "_dif"], 1)
                    nc.gpsimd.tensor_tensor(w[:, 2, :], a[:, :, 2], a[:, :, 5], ALU.add).then_inc(S[s + "_m2"], 1)
                    done(pool, s + "_sum", q)
                    done(pool, s + "_dif", q)
                    met()
                    nc.gpsimd.tensor_scalar(w[:, 3:5, :], w[:, 0:2, :], 0.5, 0.0, ALU.mult, ALU.add)\
                        .then_inc(S[s + "_half"], 1)
                    done(pool, s + "_m2", q)
                    met()
                    nc.gpsimd.tensor_scalar(w[:, 6, :], w[:, 2, :], 1.0 / C, eps, ALU.mult, ALU.add).then_inc(S[s + "_v"], 1)
                    done(pool, s + "_half", q)
                    nc.gpsimd.tensor_tensor(w[:, 5, :], w[:, 4, :], w[:, 4, :], ALU.mult).then_inc(S[s + "_d2"], 1)
                    done(pool, s + "_d2", q)
                    done(pool, s + "_v", q)
                    nc.gpsimd.tensor_tensor(w[:, 7, :], w[:, 5, :], w[:, 6, :], ALU.add).then_inc(S[s + "_var"], 1)
                    done(pool, s + "_var", q)
                    nc.gpsimd.tensor_tensor(w[:, 8, :], w[:, 7, :], halfpow[0:TN, 0:T], ALU.pow).then_inc(S[s + "_rstd"], 1)
                return step

            def center_squares(k, q, place, use, last):
                b = k % 2
                done(pool, "cen_bd", q)
                done(pool, "q_ps", q - 2)
                v = cbd[:, b, :, :, :].rearrange("c k h m -> c (k h m)")
                nc.gpsimd.tensor_tensor(csq[:, b, :], v, v, ALU.mult).then_inc(S["cen_sq"], 1)

            def center_norms(k, q, place, use, last):
                b = k % 2
                done(pool, "cen_n2", q)
                done(pool, "q_done", q - 2)
                nc.gpsimd.tensor_tensor(cinv[:, b, :], cn2[:, b, :], halfpow[0:C + 1, :], ALU.pow).then_inc(S["cen_inv"], 1)

            def token_norms(k, q, place, use, last):
                b = k % 2
                done(pool, "n2_done", q)
                met()
                nc.gpsimd.tensor_scalar(n2c[:, b, :], n2[:, b, :], NORM_FLOOR, 0.0, ALU.max, ALU.add)\
                    .then_inc(S["n2_floor"], 1)
                done(pool, "n2_floor", q)
                done(pool, "cos_done", q - 2)
                nc.gpsimd.tensor_tensor(ninv[:, b, :], n2c[:, b, :], halfpow[0:TN, 0:T * HEADS], ALU.pow)\
                    .then_inc(S["n_inv"], 1)

            def over_partitions(n, i):
                pool.wait_ge(g_max, n)
                met()
                nc.gpsimd.partition_all_reduce(gam[:, i, 1:2], gam[:, i, 0:1], 128, MAX).then_inc(g_all, 1)

            def gather(k, q, place, use, last):
                if k % 2 == 0:
                    pool.wait_ge(x_in[k // 2], use * 16 + 16)
                done(pool, "x_T", q - 2)
                met()
                nc.gpsimd.tensor_copy(xq[:, k % 2, :].rearrange("c (r w) -> c r w", w=QS), image_rows(k))\
                    .then_inc(S["x_side"], 1)

            def place_t(k, q, place, use, last):
                done(pool, "t_done", q)
                met()
                nc.gpsimd.tensor_copy(image_rows(k), tq[:, k % 2, :].rearrange("c (r w) -> c r w", w=QS))\
                    .then_inc(S["t_placed"], 1)

            attention = [(0, gather), (0, moments("x", EPS_C)), (4, moments("t", EPS_T)), (3, place_t), (0, center_squares),
                         (1, token_norms), (0, center_norms)]
            with pool.Fori(0, GROUPS) as g:
                pipeline(pool, g, attention, BODIES)
                over_partitions(2 * g + 1, 0)
                over_partitions(2 * g + 2, 1)
            pipeline(pool, GROUPS, [a for a in attention if a[0] < 4], 1)

        @block.scalar
        def _(act):
            def copy_x(k, q, place, use, last):
                done(act, "xn_ps", q)
                done(act, "s_ps", q - 2)
                nc.scalar.copy(xn[:, k % 2, 0:NA], bank(0, C + 1, NA))
                nc.scalar.copy(xn[:, k % 2, NA:QN], bank(1, C + 1, NB)).then_inc(S["xn_copied"], 1)

            def squares(t0, t1):
                def step(k, q, place, use, last):
                    if t0 == 0:
                        done(act, "n2_done", q - 1)
                    for t in range(t0, t1):
                        act.wait_ge(f_ps, q * T + (START + t + 1))
                        nc.scalar.activation(sq[:, t, :], bank(2 + t % 2, TN, D), ACT.Square).then_inc(f_sq, 1)
                return step

            def sigmoid(k, q, place, use, last):
                done(act, "cos_done", q)
                done(act, "sim_done", q - 2)
                nc.scalar.activation(sig[:, k % 2, :], cosb[:, :], ACT.Sigmoid, bias=betac[:, :]).then_inc(S["sig_done"], 1)

            def copy_eq(k, q, place, use, last):
                done(act, "eqT_ps", q)
                done(act, "first_ps", q - 1)
                nc.scalar.copy(eqT[:, :], ps[:, 2, :].bitcast(bf16)[:, 0:QN]).then_inc(S["eqT_copied"], 1)

            def copy_sim(k, q, place, use, last):
                done(act, "simT_ps", q)
                done(act, "o_ps", q - 1)
                nc.scalar.copy(simT[:, 0:NA], bank(4, HM, NA))
                nc.scalar.copy(simT[:, NA:QN], bank(5, HM, NB)).then_inc(S["simT_copied"], 1)

            def n_high():
                def step(k, q, place, use, last):
                    done(act, "n_ps", q)
                    o = tok[:, bass.ds(place, 1), 0, :].rearrange("p a n -> p (a n)")
                    nc.scalar.copy(o[:, 0:NA], bank(6, C + 2, NA))
                    nc.scalar.copy(o[:, NA:QN], bank(7, C + 2, NB)).then_inc(S["n_hi"], 1)
                return step

            def attention(g):
                return [(2, copy_eq), (3, copy_sim), (1, squares(0, TA)), (0, copy_x), (1, squares(TA, T)),
                        (4, n_high()), (1, sigmoid)]

            act.wait_ge(w_loaded, 16 * LOADS)
            with act.Fori(0, GROUPS) as g:
                pipeline(act, g, attention(g), BODIES)
                tile0 = g * (2 * GQ)

                def gelu(i, s):
                    act.wait_ge(bh_ps, i + (START + 1))
                    act.wait_ge(b_lo, i + (START - 1))
                    nc.scalar.activation(gel[:, s, :].rearrange("p (c n) -> p c n", c=FC), ps[:, 3 * s:3 * s + 3, 0:HT],
                                         ACT.Gelu, scale=scale[:, 0:1]).then_inc(b_gelu, 1)

                def y_out(i, place, s):
                    act.wait_ge(by_ps, i + (START + 1))
                    o = y32[0:C, bass.ds(place, 1), s * HT:(s + 1) * HT].rearrange("c a n -> c (a n)")
                    nc.scalar.activation(o, bank(6 + s, C, HT), ACT.Identity, bias=b2c[:, :]).then_inc(b_y, 1)

                act.wait_ge(g_scale, 2 * g + 1)
                gelu(tile0, 0)
                with act.Fori(0, GQ - 1) as p:
                    i = tile0 + 2 * p
                    gelu(i + 1, 1)
                    y_out(i, p, 0)
                    gelu(i + 2, 0)
                    y_out(i + 1, p, 1)
                i = tile0 + (2 * GQ - 2)
                gelu(i + 1, 1)
                y_out(i, GQ - 1, 0)
                y_out(i + 1, GQ - 1, 1)
            pipeline(act, GROUPS, [a for a in attention(GROUPS) if a[0] < 4], 1)

        @block.vector
        def _(dve):
            count = [0]

            def step(ins):
                count[0] += 1
                ins.then_inc(dve_set, 1)
                dve.wait_ge(dve_set, count[0])

            v = nc.vector
            dve.wait_ge(w_loaded, 16 * LOADS)
            dve.wait_ge(pool_set, POOL_SETS)
            step(v.tensor_copy(ident16[:, :], ident))
            step(v.tensor_copy(first16[:, :], const("first")))
            for w, gt, total, mean, n in ((w1, gt1, wsum1, wmean1, G1 * C), (w2, gt2, wsum2, wmean2, G2 * F)):
                step(v.reduce_sum(total[:, :], w[:, :, :], AX.X))
            assert count[0] == DVE_SUMS
            dve.wait_ge(pe_set, 1)
            step(v.tensor_scalar(wmean1[:, :], bank(0, G1, GROUPS), 1.0 / (G1 * C), None, ALU.mult))
            step(v.tensor_scalar(wmean2[:, :], bank(1, G2, GROUPS), 1.0 / (G2 * F), None, ALU.mult))
            for w, gt, mean, rows, n in ((w1, gt1, wmean1, G1, C), (w2, gt2, wmean2, G2, F)):
                m = mean[:, :].unsqueeze(2).broadcast_to([rows, GROUPS, n])
                step(v.tensor_tensor(gt[:, :, :], w[:, :, :], m, ALU.is_gt))
                step(v.tensor_tensor(w[:, :, :], w[:, :, :], m, ALU.is_lt))
                step(v.tensor_tensor(w[:, :, :], gt[:, :, :], w[:, :, :], ALU.subtract))
            step(v.tensor_copy(wfT[:, :], bank(2, C + 1, D)))
            wpT = bank(3, C, D).rearrange("r (k o) -> r k o", k=4)
            for h in range(2):
                step(v.tensor_scalar(wph[:, :, h, :], wpT, const("head_of_row", C)[:, h:h + 1], None, ALU.mult))
            step(v.tensor_copy(V[:, :, 2 * C:VN], const("last_row", C + 1).unsqueeze(1).broadcast_to([C + 1, 4, 2])))
            r, m = slice(C, C + 2), const("bias_part")
            step(v.tensor_copy(b1h[r, :], b1s[r, :]))
            step(v.tensor_tensor(b1l[r, :], b1s[r, :], b1h[r, :], ALU.subtract))
            step(v.tensor_scalar(b1l[r, :], b1l[r, :], m[r, 1:2], None, ALU.mult))
            step(v.scalar_tensor_tensor(w1T[r, :], b1h[r, :], m[r, 0:1], b1l[r, :], ALU.mult, ALU.add))
            assert count[0] == DVE_SIGNS
            dve.wait_ge(pe_set, 2)
            for i in range(2):
                step(v.tensor_copy(V[:, 2 * i:2 * i + 2, 0:2 * C],
                                   bank(4 + i, C + 1, 4 * C).rearrange("c (k o) -> c k o", k=2)))
            step(v.tensor_copy(w1T[0:C, 0:G1 * GROUPS], bank(6, C, G1 * GROUPS)))
            step(v.tensor_copy(w2T[:, :, 0:G2 * GROUPS],
                               bank(7, 128, FC * C).rearrange("f (c o) -> f c o", c=FC)[:, :, 0:G2 * GROUPS]))
            assert count[0] == DVE_ALL

            def stats(s, b0):
                def step(k, q, place, use, last):
                    done(dve, s + "_T", q)
                    done(dve, s + "_rstd", q - 2)
                    for t in range(T):
                        src = bank(b0, TN, C, t * C) if t < TA else bank(b0 + 1, TN, C, (t - TA) * C)
                        last_one = v.bn_stats(st[s][:, k % 2, t, :], src)
                    last_one.then_inc(S[s + "_stats"], 1)
                return step

            def normalise(s, b0):
                def step(k, q, place, use, last):
                    done(dve, s + "_rstd", q)
                    if s == "x":
                        done(dve, "u_ps", q - 4)
                    else:
                        done(dve, "n_ps", q - 2)
                    m = mo[s][:, k % 2, :, :]
                    for t in range(T):
                        src = bank(b0, TN, C, t * C) if t < TA else bank(b0 + 1, TN, C, (t - TA) * C)
                        dst = xnT[:, k % 4, t, 0:C] if s == "x" else nT[:, k % 2, t, 0:C]
                        last_one = v.tensor_scalar(dst, src, m[:, 3, t:t + 1], m[:, 8, t:t + 1], ALU.subtract, ALU.mult)
                    last_one.then_inc(S[s + "_norm"], 1)
                return step

            def pooled(k, q, place, use, last):
                done(dve, "xn_ps", q)
                done(dve, "xn_copied", q)
                done(dve, "u_done", q - 4)
                v.tensor_scalar(cenx[:, k % 4, :], bank(1, C + 1, CENTERS, NB), 1.0 / (PW * PW), None, ALU.mult)\
                    .then_inc(S["cen_x"], 1)

            def centers(k, q, place, use, last):
                done(dve, "cen_f", q)
                done(dve, "q_ps", q - 2)
                f = bank(0, C, 4 * CENTERS).rearrange("r (k m) -> r k m", k=4)
                mask = const("head_of_row", C)
                v.tensor_tensor(cbd[:, k % 2, :, :, :], f.unsqueeze(2).broadcast_to([C, 4, 2, CENTERS]),
                                mask.unsqueeze(1).unsqueeze(3).broadcast_to([C, 4, 2, CENTERS]), ALU.mult)\
                    .then_inc(S["cen_bd"], 1)

            def center_floor(k, q, place, use, last):
                done(dve, "q_ps", q)
                done(dve, "cen_inv", q - 2)
                v.tensor_scalar(cn2[:, k % 2, :], bank(0, C + 1, HM, 128), NORM_FLOOR, None, ALU.max)\
                    .then_inc(S["cen_n2"], 1)

            def q_scaled(k, q, place, use, last):
                done(dve, "cen_inv", q)
                done(dve, "s_ps", q - 2)
                v.scalar_tensor_tensor(Q[:, k % 2, :], bank(0, C + 1, HM, 256), alphac[:, :], cinv[:, k % 2, :],
                                       ALU.mult, ALU.mult).then_inc(S["q_done"], 1)

            def norms(t0, t1):
                def step(k, q, place, use, last):
                    dve.wait_ge(f_sq, q * T + (START + t1))
                    if t0 == 0:
                        done(dve, "n2_floor", q - 2)
                    ins = v.reduce_sum(n2[:, k % 2, t0 * HEADS:t1 * HEADS],
                                       sq[:, t0:t1, :].rearrange("p t (h d) -> p (t h) d", d=HD), AX.X)
                    if t1 == T:
                        ins.then_inc(S["n2_done"], 1)
                return step

            def heads(ap):
                return ap.rearrange("p (h m) -> p h m", m=CENTERS)

            def over_centers(ap):
                return ap.unsqueeze(2).broadcast_to([TN, T * HEADS, CENTERS])

            def cosine(k, q, place, use, last):
                done(dve, "s_ps", q)
                done(dve, "n_inv", q)
                done(dve, "sig_done", q - 1)
                v.tensor_tensor(heads(cosb[:, :]), heads(pair(2, TN, T * HM)), over_centers(ninv[:, k % 2, :]), ALU.mult)\
                    .then_inc(S["cos_done"], 1)

            def first_marks(k, q, place, use, last):
                done(dve, "sig_done", q)
                v.tensor_reduce(top[:, :], heads(sig[:, k % 2, :]), AX.X, ALU.max).then_inc(S["top_done"], 1)
                done(dve, "top_done", q)
                done(dve, "eqT_ps", q - 1)
                v.tensor_tensor(heads(eq[:, :]), heads(sig[:, k % 2, :]), over_centers(top[:, :]), ALU.is_equal)\
                    .then_inc(S["eq_done"], 1)

            def masked(k, q, place, use, last):
                done(dve, "first_ps", q)
                done(dve, "u_ps", q - 2)
                v.scalar_tensor_tensor(sim[:, k % 2, :], pair(2, TN, T * HM), -1.0, sig[:, k % 2, :],
                                       ALU.is_equal, ALU.mult).then_inc(S["sim_done"], 1)

            def summed(k, q, place, use, last):
                done(dve, "u_ps", q)
                done(dve, "a_ps", q - 1)
                v.tensor_tensor(heads(uT[:, :]), heads(bank(4, C + 1, HM)),
                                cenx[:, k % 4, :].unsqueeze(1).broadcast_to([C + 1, HEADS, CENTERS]), ALU.add)\
                    .then_inc(S["u_done"], 1)

            def aggregated(k, q, place, use, last):
                done(dve, "a_ps", q)
                v.reciprocal(rden[:, :], bank(5, HM, 1, 2 * C)).then_inc(S["a_rden"], 1)
                done(dve, "a_rden", q)
                v.tensor_scalar(hmul[:, :], const("head_of_center"), rden[:, :], None, ALU.mult).then_inc(S["a_mul"], 1)
                done(dve, "a_mul", q)
                v.tensor_scalar(a1[:, :], bank(5, HM, C), hmul[:, 0:1], None, ALU.mult).then_inc(S["a_half"], 1)
                done(dve, "a_half", q)
                done(dve, "o_ps", q - 1)
                v.scalar_tensor_tensor(aggp[:, :], bank(5, HM, C, C), hmul[:, 1:2], a1[:, :], ALU.mult, ALU.add)\
                    .then_inc(S["a_done"], 1)

            def residual(k, q, place, use, last):
                done(dve, "o_ps", q)
                if with_ffn[0]:
                    done(dve, "t_T", q - 2)
                done(dve, "t_placed", q - 2)
                for b, lo, n in ((4, 0, NA // QS), (5, NA // QS, NB // QS)):
                    o = bank(b, C, n * QS).rearrange("c (r w) -> c r w", w=QS)
                    t = tq[:, k % 2, lo * QS:(lo + n) * QS].rearrange("c (r w) -> c r w", w=QS)
                    ins = v.scalar_tensor_tensor(t, o, bpc[:, :], image_rows(k, lo, n), ALU.add, ALU.add)
                ins.then_inc(S["t_done"], 1)

            def n_low():
                def step(k, q, place, use, last):
                    done(dve, "n_hi", q)
                    hi, lo = (tok[:, bass.ds(place, 1), i, :].rearrange("p a n -> p (a n)") for i in range(2))
                    v.tensor_tensor(lo[:, 0:NA], bank(6, C + 2, NA), hi[:, 0:NA], ALU.subtract)
                    v.tensor_tensor(lo[:, NA:QN], bank(7, C + 2, NB), hi[:, NA:QN], ALU.subtract).then_inc(S["n_lo"], 1)
                return step

            def h_largest(u0, u1):
                def step(k, q, place, use, last):
                    for u in range(u0, u1):
                        dve.wait_ge(h_ps, q * (2 * FC) + (START + u + 1))
                        o = hmax[:, bass.ds(place * (2 * FC) + u, 1)]
                        v.tensor_reduce(o, bank(6 + u % 2, 128, HT), AX.X, ALU.max, apply_absolute_value=True)\
                            .then_inc(h_max, 1)
                return step

            with_ffn = [True]

            def attention(g):
                return [(0, stats("x", 0)), (2, masked), (3, summed), (4, stats("t", 6)), (3, aggregated), (1, norms(0, TA)),
                        (0, normalise("x", 0)), (0, pooled), (3, residual), (1, norms(TA, T)), (4, normalise("t", 6)),
                        (4, n_low()), (0, centers), (5, h_largest(0, FC)), (0, center_floor), (1, cosine),
                        (0, q_scaled), (5, h_largest(FC, 2 * FC)), (1, first_marks)]

            def largest(src, n, i, rows):
                v.tensor_reduce(gam[0:rows, i, 0:1], src, AX.X, ALU.max).then_inc(g_max, 1)
                dve.wait_ge(g_all, n)
                v.tensor_scalar(den[:, i, 0:1], gam[:, i, 1:2], EPS_Q, None, ALU.add).then_inc(g_eps, 1)
                dve.wait_ge(g_eps, n)
                v.reciprocal(den[:, i, 1:2], den[:, i, 0:1]).then_inc(g_rec, 1)
                dve.wait_ge(g_rec, n)
                v.tensor_scalar(scale[:, i:i + 1], den[:, i, 1:2], QB, None, ALU.mult).then_inc(g_scale, 1)
                dve.wait_ge(g_scale, n)
                dve.sem_inc(waited, 1)

            with dve.Fori(0, GROUPS) as g:
                pipeline(dve, g, attention(g), BODIES)
                dve.wait_ge(h_max, g * (GQ * 2 * FC) + (START + GQ * 2 * FC))
                largest(hmax[:, :], 2 * g + 1, 0, 128)
                tile0 = g * (2 * GQ)

                def split(i, s):
                    dve.wait_ge(b_gelu, i + (START + 1))
                    dve.wait_ge(by_ps, i + (START - 1))
                    v.tensor_scalar(ghi[:, s, :], gel[:, s, :], QCLIP, None, ALU.min).then_inc(b_hi, 1)
                    dve.wait_ge(b_hi, i + (START + 1))
                    v.scalar_tensor_tensor(glo[:, s, :], gel[:, s, :], QCLIP, ghi[:, s, :], ALU.min, ALU.subtract)\
                        .then_inc(b_lo, 1)

                def y_largest(i, place, s):
                    dve.wait_ge(b_y, i + (START + 1))
                    y = y32[0:C, bass.ds(place, 1), s * HT:(s + 1) * HT].rearrange("c a n -> c (a n)")
                    v.tensor_reduce(ymax[:, bass.ds(2 * place + s, 1)], y, AX.X, ALU.max, apply_absolute_value=True)\
                        .then_inc(b_ymax, 1)

                split(tile0, 0)
                with dve.Fori(0, GQ - 1) as p:
                    i = tile0 + 2 * p
                    split(i + 1, 1)
                    y_largest(i, p, 0)
                    split(i + 2, 0)
                    y_largest(i + 1, p, 1)
                i = tile0 + (2 * GQ - 2)
                split(i + 1, 1)
                y_largest(i, GQ - 1, 0)
                y_largest(i + 1, GQ - 1, 1)
                dve.wait_ge(b_ymax, g * (2 * GQ) + (START + 2 * GQ))
                largest(ymax[:, :], 2 * g + 2, 1, C)

                with dve.Fori(0, BODIES) as b:
                    for k in range(BODY):
                        q = g * GQ + b * BODY + k
                        if k % 2 == 0:
                            dve.wait_ge(x_in[k // 2], (g * (2 * BODIES) + b) * 16 + (BODIES + 1) * 16)
                        y = y32[0:C, bass.ds(b * BODY + k, 1), :].rearrange("c a n -> c (a n)")
                        v.tensor_scalar(y, y, scale[0:C, 1:2], QCLIP, ALU.mult, ALU.min).then_inc(S["c_min"], 1)
                        done(dve, "c_min", q)
                        ins = v.scalar_tensor_tensor(image_rows(k), y.rearrange("c (r w) -> c r w", w=QS), -QCLIP,
                                                     image_rows(k), ALU.max, ALU.add)
                        if k % 2 == 1:
                            ins.then_inc(c_half, 1)
            with_ffn[0] = False
            pipeline(dve, GROUPS, [a for a in attention(GROUPS) if a[0] < 4], 1)

        @block.tensor
        def _(pe):
            mm, tr = nc.tensor.matmul, nc.tensor.transpose
            pe.wait_ge(w_loaded, 16 * LOADS)
            pe.wait_ge(dve_set, DVE_SUMS)
            mm(bank(0, G1, GROUPS), ones[0:G1, 0:G1], wsum1[:, :], start=True, stop=True)
            mm(bank(1, G2, GROUPS), ones[0:G2, 0:G2], wsum2[:, :], start=True, stop=True)
            for k in range(4):
                tr(bank(2, C + 1, C, k * C), wf[:, k, :], ident[0:C, 0:C])
                ins = tr(bank(3, C, C, k * C), wp[:, k * C:(k + 1) * C], ident[0:C, 0:C])
            ins.then_inc(pe_set, 1)
            pe.wait_ge(dve_set, DVE_SIGNS)
            for k in range(4):
                mm(bank(4 + k // 2, C + 1, 2 * C, k % 2 * 2 * C), wv[:, k, :],
                   wph[:, k, :, :].rearrange("r h o -> r (h o)"), start=True, stop=True)
            for g in range(GROUPS):
                tr(bank(6, C, G1, g * G1), w1[:, g, :], ident[0:G1, 0:G1])
                for c in range(FC):
                    ins = tr(bank(7, 128, G2, c * C + g * G2), w2[:, g, c * 128:(c + 1) * 128], ident[0:G2, 0:G2])
            ins.then_inc(pe_set, 1)
            pe.wait_ge(dve_set, DVE_ALL)

            def tile_bank(b0, rows, n, t):
                return bank(b0, rows, n, t * n) if t < TA else bank(b0 + 1, rows, n, (t - TA) * n)

            def to_tokens(s, b0):
                def step(k, q, place, use, last):
                    if s == "x":
                        done(pe, "x_side", q)
                        done(pe, "q_done", q - 1)
                    else:
                        done(pe, "t_done", q)
                        pe.wait_ge(h_max, q * (2 * FC) + (START - 2 * FC))
                    for t in range(T):
                        src = (xq if s == "x" else tq)[:, k % 2, t * TN:(t + 1) * TN]
                        ins = tr(tile_bank(b0, TN, C, t), src, ident[0:C, 0:C])
                    ins.then_inc(S[s + "_T"], 1)
                return step

            def x_back(k, q, place, use, last):
                done(pe, "x_norm", q)
                for t in range(T):
                    mm(bank(1, C + 1, CENTERS, NB), xnT[:, k % 4, t, :], poolm[:, t, :], start=t == 0, stop=t == T - 1)
                for t in range(T):
                    ins = tr(tile_bank(0, C + 1, TN, t), xnT[:, k % 4, t, :], ident[0:TN, 0:TN])
                ins.then_inc(S["xn_ps"], 1)

            def centers(k, q, place, use, last):
                done(pe, "cen_x", q)
                done(pe, "xn_copied", q)
                for c in range(4):
                    ins = mm(bank(0, C, CENTERS, c * CENTERS), wfT[:, c * C:(c + 1) * C], cenx[:, k % 4, :],
                             start=True, stop=True)
                ins.then_inc(S["cen_f"], 1)

            def center_products(k, q, place, use, last):
                done(pe, "cen_bd", q)
                done(pe, "cen_sq", q)
                mm(bank(0, C + 1, HM, 128), ones[0:C, 0:C + 1], csq[:, k % 2, :], start=True, stop=True)
                for c in range(4):
                    n = 2 * CENTERS
                    ins = mm(bank(0, C + 1, n, 256 + c * n), wf[:, c, :],
                             cbd[:, k % 2, c, :, :].rearrange("r h m -> r (h m)"), start=True, stop=True)
                ins.then_inc(S["q_ps"], 1)

            def features(t0, t1):
                def step(k, q, place, use, last):
                    if t0 == 0:
                        done(pe, "xn_copied", q)
                        done(pe, "sim_done", q - 1)
                    for t in range(t0, t1):
                        if t >= 2:
                            pe.wait_ge(f_sq, q * T + (START + t - 1))
                        mm(bank(2 + t % 2, TN, D), xn[:, k % 2, t * TN:(t + 1) * TN], wfT[:, :], start=True, stop=True)\
                            .then_inc(f_ps, 1)
                return step

            def scores(k, q, place, use, last):
                pe.wait_ge(f_sq, q * T + (START + T))
                done(pe, "q_done", q)
                for t in range(T):
                    ins = mm(tile_bank(2, TN, HM, t), xn[:, k % 2, t * TN:(t + 1) * TN], Q[:, k % 2, :],
                             start=True, stop=True)
                ins.then_inc(S["s_ps"], 1)

            def marks_back(k, q, place, use, last):
                done(pe, "eq_done", q)
                o = ps[:, 2, :].bitcast(bf16)
                for t in range(T):
                    ins = tr(o[:, t * TN:(t + 1) * TN], eq[:, t * HM:(t + 1) * HM], ident16[0:TN, 0:TN])
                ins.then_inc(S["eqT_ps"], 1)

            def find_first(k, q, place, use, last):
                done(pe, "eqT_copied", q)
                for t in range(T):
                    ins = mm(tile_bank(2, TN, HM, t), eqT[:, t * TN:(t + 1) * TN], first16[:, :], start=True, stop=True)
                ins.then_inc(S["first_ps"], 1)

            def sim_back(k, q, place, use, last):
                done(pe, "sim_done", q)
                done(pe, "t_done", q - 1)
                for t in range(T):
                    ins = tr(tile_bank(4, HM, TN, t), sim[:, k % 2, t * HM:(t + 1) * HM], ident[0:TN, 0:TN])
                ins.then_inc(S["simT_ps"], 1)

            def aggregate(k, q, place, use, last):
                done(pe, "simT_copied", q)
                for t in range(T):
                    ins = mm(bank(4, C + 1, HM), xnT[:, k % 4, t, :], sim[:, k % 2, t * HM:(t + 1) * HM],
                             start=t == 0, stop=t == T - 1)
                ins.then_inc(S["u_ps"], 1)

            def project(k, q, place, use, last):
                done(pe, "u_done", q)
                for c in range(4):
                    n = 2 * CENTERS
                    ins = mm(ps[c * n:(c + 1) * n, 5, 0:VN], uT[:, c * n:(c + 1) * n], V[:, c, :], start=True, stop=True)
                ins.then_inc(S["a_ps"], 1)

            def spread(k, q, place, use, last):
                done(pe, "a_done", q)
                mm(bank(4, C, NA), aggp[:, :], simT[:, 0:NA], start=True, stop=True)
                mm(bank(5, C, NB), aggp[:, :], simT[:, NA:QN], start=True, stop=True).then_inc(S["o_ps"], 1)

            def t_back(k, q, place, use, last):
                done(pe, "t_norm", q)
                for t in range(T):
                    ins = tr(tile_bank(6, C + 2, TN, t), nT[:, k % 2, t, :], ident[0:TN, 0:TN])
                ins.then_inc(S["n_ps"], 1)

            def hidden(dst, place, s, c):
                for part in range(2):
                    ins = mm(dst, w1T[:, c * 128:(c + 1) * 128],
                             tok[:, bass.ds(place, 1), part, s * HT:(s + 1) * HT].rearrange("p a n -> p (a n)"),
                             start=part == 0, stop=part == 1)
                return ins

            def hidden_tiles(u0, u1):
                def step(k, q, place, use, last):
                    if u0 == 0:
                        done(pe, "n_lo", q if last else q + 1)
                        if last:
                            pe.wait_ge(h_max, q * (2 * FC) + START)
                    for u in range(u0, u1):
                        if u >= 2:
                            pe.wait_ge(h_max, q * (2 * FC) + (START + u - 1))
                        hidden(bank(6 + u % 2, 128, HT), place, u // FC, u % FC).then_inc(h_ps, 1)
                return step

            def attention(g):
                return [(2, marks_back), (3, sim_back), (0, to_tokens("x", 0)), (2, find_first), (3, aggregate),
                        (4, to_tokens("t", 6)), (3, project), (1, features(0, TA)), (0, x_back), (3, spread),
                        (1, features(TA, T)), (4, t_back), (0, centers), (1, scores), (5, hidden_tiles(0, FC)),
                        (0, center_products), (5, hidden_tiles(FC, 2 * FC))]

            with pe.Fori(0, GROUPS) as g:
                pipeline(pe, g, attention(g), BODIES)
                tile0 = g * (2 * GQ)

                def up(i, place, s):
                    pe.wait_ge(b_gelu, i + (START - 1))
                    for c in range(FC):
                        ins = hidden(bank(3 * s + c, 128, HT), place, s, c)
                    ins.then_inc(bh_ps, 1)

                def down(i, s):
                    pe.wait_ge(b_lo, i + (START + 1))
                    pe.wait_ge(b_y, i + (START - 1))
                    for n, (part, c) in enumerate((part, c) for part in (ghi, glo) for c in range(FC)):
                        ins = mm(bank(6 + s, C, HT), w2T[:, c, :], part[:, s, c * HT:(c + 1) * HT],
                                 start=n == 0, stop=n == 2 * FC - 1)
                    ins.then_inc(by_ps, 1)

                pe.wait_ge(h_max, g * (GQ * 2 * FC) + (START + GQ * 2 * FC))
                up(tile0, 0, 0)
                with pe.Fori(0, GQ - 1) as p:
                    i = tile0 + 2 * p
                    up(i + 1, p, 1)
                    down(i, 0)
                    up(i + 2, p + 1, 0)
                    down(i + 1, 1)
                i = tile0 + (2 * GQ - 2)
                up(i + 1, GQ - 1, 1)
                down(i, 0)
                down(i + 1, 1)
            pipeline(pe, GROUPS, [a for a in attention(GROUPS) if a[0] < 4], 1)


INPUTS = ["x"] + ["L0_conv_" + n for n in ("Wf", "bf", "Wv", "bv", "Wp", "bp", "sim_alpha", "sim_beta")] \
    + ["L0_ffn_" + n for n in ("W1", "b1", "W2", "b2")]


def kernel(**inputs):
    import concourse.bacc as bacc
    from concourse.bass_utils import run_bass_kernel_spmd

    nc = bacc.Bacc("TRN2", target_bir_lowering=False, num_devices=1)
    arrays = {f"in_{n}": np.ascontiguousarray(inputs[n]) for n in INPUTS}
    arrays["in_constants"] = SHAPE_CONSTANTS
    args = [nc.dram_tensor(n, a.shape, mybir.dt.from_np(a.dtype), kind="ExternalInput").ap() for n, a in arrays.items()]
    args.append(nc.dram_tensor("out_0", (IMAGES, C, SIDE, SIDE), mybir.dt.float32, kind="ExternalOutput").ap())
    build(nc, *args)
    r = run_bass_kernel_spmd(nc, [arrays], core_ids=[0])
    return r.results[0]["out_0"]
```

```python
import numpy as np
import concourse.bass as bass
from concourse import mybir
from contextlib import ExitStack

IMAGES, C, SIDE = 32, 96, 56
PIX = SIDE * SIDE
QS = SIDE // 2
QN = QS * QS
HEADS, HD, CENTERS = 8, 48, 16
D = HEADS * HD
HM = HEADS * CENTERS
ROWS_T = 4
T = QS // ROWS_T
TN = ROWS_T * QS
PW = QS // 4
HALF = PIX // 2
TA = 4
NA, NB = TA * TN, (T - TA) * TN
GROUPS, GSIZE = 5, IMAGES // 5
GQ = GSIZE * 4
XB = 4
BODY = 2 * XB
BODIES = GQ // BODY
F = 4 * C
FC = F // 128
G1, G2 = F // GROUPS, C // GROUPS
HT = QN // 2
VN = 2 * C + 2
EPS_C, EPS_T, EPS_Q, QB = 1e-6, 1e-5, 1e-5, 128.0
QCLIP = float(np.float32(QB - EPS_Q))
NORM_FLOOR = 1e-24
START = 16
LOADS = 14
POOL_SETS = 6
DVE_SUMS, DVE_SIGNS, DVE_ALL = 4, 20, 24
CONSTS = {}


def shape_constants():
    parts = {"ident": np.eye(128), "ones": np.ones((128, 128))}
    j, m = np.meshgrid(np.arange(HM), np.arange(HM), indexing="ij")
    same = j // CENTERS == m // CENTERS
    parts["first"] = np.where(same & (j < m), 1.0, 0.0) - np.eye(HM)
    pool = np.zeros((128, T, CENTERS))
    for t in range(T):
        for p in range(TN):
            row, col = ROWS_T * t + p // QS, p % QS
            pool[p, t, row // PW * 4 + col // PW] = 1.0
    parts["pool"] = pool.reshape(128, -1)
    p = np.arange(128)
    parts["head_of_row"] = np.stack([p < HD, (p >= HD) & (p < 2 * HD)], 1)
    parts["head_of_center"] = np.stack([p // CENTERS % 2 == 0, p // CENTERS % 2 == 1], 1)
    parts["bias_part"] = np.stack([p == C, p == C + 1], 1)
    parts["last_row"] = np.stack([p == C, p == C], 1)
    at = 0
    for name, a in parts.items():
        CONSTS[name] = (at, a.shape[1])
        at += a.shape[1]
    return np.concatenate([a.astype(np.float32) for a in parts.values()], 1)


SHAPE_CONSTANTS = shape_constants()


def build(nc, x, Wf, bf, Wv, bv, Wp, bp, alpha, beta, W1, b1, W2, b2, consts, out):
    f32, f16, bf16 = mybir.dt.float32, mybir.dt.float16, mybir.dt.bfloat16
    ALU, ACT, AX = mybir.AluOpType, mybir.ActivationFunctionType, mybir.AxisListType
    MAX = bass.bass_isa.ReduceOp.max
    ctx = ExitStack()
    with ctx:
        def sb(name, shape, dt=f32):
            return ctx.enter_context(nc.sbuf_tensor(name, shape, dt))

        def sem(name):
            return ctx.enter_context(nc.semaphore(name))

        ps = ctx.enter_context(nc.psum_tensor("ps", [128, 8, 512], f32))

        xbuf = sb("xbuf", [C, XB, HALF])
        tok = sb("tok", [C + 2, GQ, 2, QN], f16)
        xq = sb("xq", [C, 2, QN])
        tq = sb("tq", [C, 2, QN])
        xnT = sb("xnT", [TN, 4, T, C + 1])
        xn = sb("xn", [C + 1, 2, QN])
        cenx = sb("cenx", [C + 1, 4, CENTERS])
        cbd = sb("cbd", [C, 2, 4, 2, CENTERS])
        csq = sb("csq", [C, 2, HM])
        cn2 = sb("cn2", [HM, 2])
        cinv = sb("cinv", [HM, 2])
        qT = sb("qT", [HM, C + 1])
        Q = sb("Q", [C + 1, 2, HM])
        sq = sb("sq", [TN, T, D])
        n2 = sb("n2", [TN, T * HEADS])
        n2c, ny2, nxy = (sb(n, [TN, T * HEADS]) for n in ("n2c", "ny2", "nxy"))
        ninv = sb("ninv", [TN, T * HEADS])
        cosb = sb("cosb", [TN, T * HM])
        sig = sb("sig", [TN, 2, T * HM])
        top = sb("top", [TN, T * HEADS])
        eq = sb("eq", [TN, T * HM], bf16)
        eqT = sb("eqT", [HM, QN], bf16)
        sim = sb("sim", [TN, 2, T * HM])
        simT = sb("simT", [HM, QN])
        uT = sb("uT", [C + 1, HM])
        rden = sb("rden", [HM, 1])
        hmul = sb("hmul", [HM, 2])
        a1 = sb("a1", [HM, C])
        aggp = sb("aggp", [HM, C])
        nT = sb("nT", [TN, 2, T, C + 2])
        st = {s: sb(f"st_{s}", [TN, 2, T, 6]) for s in "xt"}
        mo = {s: sb(f"mo_{s}", [TN, 2, 10, T]) for s in "xt"}
        hmax = sb("hmax", [128, GQ * 2 * FC])
        ymax = sb("ymax", [C, GQ * 2])
        gam = sb("gam", [128, 2, 2])
        den = sb("den", [128, 2, 2])
        scale = sb("scale", [128, 2])
        gel = sb("gel", [128, 2, FC * HT])
        ghi = sb("ghi", [128, 2, FC * HT], f16)
        glo = sb("glo", [128, 2, FC * HT], f16)
        cst = sb("cst", [128, SHAPE_CONSTANTS.shape[1]])
        ident16 = sb("ident16", [128, 128], bf16)
        first16 = sb("first16", [HM, HM], bf16)
        halfpow = sb("halfpow", [128, HM])
        wf = sb("wf", [C, 4, C + 1])
        wfT = sb("wfT", [C + 1, D])
        V = sb("V", [C + 1, 4, VN])
        b1h = sb("b1h", [C + 2, F], f16)
        wsum1, wsum2 = sb("wsum1", [G1, GROUPS]), sb("wsum2", [G2, GROUPS])
        wmean1, wmean2 = sb("wmean1", [G1, GROUPS]), sb("wmean2", [G2, GROUPS])
        w1T = sb("w1T", [C + 2, F], f16)
        w2T = sb("w2T", [128, FC, C], f16)
        b2c, bpc = sb("b2c", [C, 1]), sb("bpc", [C, 1])
        alphac, betac = sb("alphac", [HM, 1]), sb("betac", [TN, 1])

        def const(name, rows=128):
            at, n = CONSTS[name]
            return cst[0:rows, at:at + n]

        def bank(b, rows, n, at=0):
            return ps[0:rows, b, at:at + n]

        def pair(b, rows, n):
            return ps[0:rows, b:b + 2, :].rearrange("p b n -> p (b n)")[:, 0:n]

        ident, ones = const("ident"), const("ones")
        poolm = const("pool", TN).rearrange("p (t m) -> p t m", t=T)
        y32 = tok[:, :, :, :].rearrange("p q s n -> p (q s n)").bitcast(f32).rearrange("p (q n) -> p q n", n=QN)

        room = [0]

        def early(rows, *shape):
            n = int(np.prod(shape))
            a = y32.rearrange("p q n -> p (q n)")[0:rows, room[0]:room[0] + n]
            room[0] += n
            names = "abc"[:len(shape)]
            return a.rearrange(f"p ({' '.join(names)}) -> p {' '.join(names)}", **dict(zip(names, shape)))

        wv, wp = early(C, 4, C + 1), early(C, D)
        wph = early(C, 4, 2, C)
        w1, gt1, w2, gt2 = early(G1, GROUPS, C), early(G1, GROUPS, C), early(G2, GROUPS, F), early(G2, GROUPS, F)
        b1s, b1l = early(C + 2, F), early(C + 2, F)

        NAMES = """x_side x_T x_stats x_sum x_dif x_m2 x_half x_d2 x_v x_var x_rstd x_shift x_norm xn_ps xn_copied cen_x cen_f cen_bd
            cen_sq q_ps cen_n2 cen_inv q_scaled q_T q_done s_ps n2_done n2_floor n_guess n_square0 n_part0 n_factor0 n_newton0
            n_square1 n_part1 n_factor1 n_newton1 n_square2 n_part2 n_factor2 n_newton2 cos_done sig_done top_done eq_done
            eqT_ps eqT_copied first_ps sim_done simT_ps simT_copied u_ps u_done a_ps a_rden a_mul a_half a_done o_ps t_done t_placed
            t_T t_stats t_sum t_dif t_m2 t_half t_d2 t_v t_var t_rstd t_shift t_norm n_ps n_hi n_lo c_min c_max""".split()
        S = {n: sem("s_" + n) for n in NAMES}
        f_ps, f_sq = sem("f_ps"), sem("f_sq")
        h_ps, h_max = sem("h_ps"), sem("h_max")
        bh_ps, b_gelu, b_hi, b_lo, by_ps, b_y, b_ymax = (
            sem(n) for n in ("bh_ps", "b_gelu", "b_hi", "b_lo", "by_ps", "b_y", "b_ymax"))
        STARTED = list(S.values()) + [f_ps, f_sq, h_ps, h_max, bh_ps, b_gelu, b_hi, b_lo, by_ps, b_y, b_ymax]
        x_in = [sem(f"x_in{j}") for j in range(XB)]
        t_out = [sem(f"t_out{j}") for j in range(XB)]
        waited = sem("waited")
        c_half = sem("c_half")
        g_max, g_all, g_eps, g_rec, g_scale = (sem(n) for n in ("g_max", "g_all", "g_eps", "g_rec", "g_scale"))
        w_loaded, pe_set, dve_set, pool_set = sem("w_loaded"), sem("pe_set"), sem("dve_set"), sem("pool_set")

        def done(eng, name, q):
            eng.wait_ge(S[name], q + (START + 1))

        FFN = True

        def pipeline(eng, g, steps, bodies, ffn=True):
            steps = [s[:2] for s in steps if ffn or s[-1] is not FFN]

            def slots(js, first, use, filled, tail):
                for j in js:
                    for lag, step in steps:
                        d = j - lag
                        if (d >= 0 or filled) and not (tail and d >= BODY):
                            step(d % BODY, g * GQ + first + d, first + d, use, tail and d == BODY - 1)
            use = g * (2 * BODIES)
            slots(range(BODY), 0, use, False, False)
            if bodies > 1:
                with eng.Fori(1, bodies) as b:
                    slots(range(BODY), b * BODY, use + b, True, False)
            slots(range(BODY, BODY + max(lag for lag, _ in steps)), (bodies - 1) * BODY, use, True, True)

        def image_rows(k, lo=0, n=QS):
            v = xbuf[:, k // 2, :].rearrange("c (r w) -> c r w", w=SIDE)
            return v[:, lo:lo + n, k % 2 * QS:(k % 2 + 1) * QS]

        block = ctx.enter_context(nc.Block())

        @block.sync
        def _(sp):
            for s in STARTED:
                sp.sem_inc(s, START)
            per_row = [(cst[:, :], consts), (w1[:, :, :], W1[0:G1 * GROUPS, :].rearrange("(g r) c -> r g c", g=GROUPS)),
                       (w2[:, :, :], W2[0:G2 * GROUPS, :].rearrange("(g r) f -> r g f", g=GROUPS)),
                       (wf[:, :, 0:C], Wf.rearrange("(k r) c -> r k c", k=4)),
                       (wv[:, :, 0:C], Wv.rearrange("(k r) c -> r k c", k=4)),
                       (wf[:, :, C:C + 1], bf.rearrange("(k r a) -> r k a", k=4, a=1)),
                       (wv[:, :, C:C + 1], bv.rearrange("(k r a) -> r k a", k=4, a=1)),
                       (wp[:, :], Wp),
                       (b1s[C:C + 1, :], b1.rearrange("(a f) -> a f", a=1)),
                       (b1s[C + 1:C + 2, :], b1.rearrange("(a f) -> a f", a=1)),
                       (b2c[:, :], b2.rearrange("(c a) -> c a", a=1)), (bpc[:, :], bp.rearrange("(c a) -> c a", a=1)),
                       (alphac[:, :], alpha.rearrange("(c a) -> c a", a=1).broadcast_to([HM, 1])),
                       (betac[:, :], beta.rearrange("(c a) -> c a", a=1).broadcast_to([TN, 1]))]
            assert len(per_row) == LOADS
            with nc.allow_non_contiguous_dma(reason="a bias as a column: a few hundred numbers"):
                for dst, src in per_row:
                    sp.dma_start(dst, src).then_inc(w_loaded, 16)

            x_half = x.rearrange("i c (s h) w -> i s c (h w)", s=2)
            o_half = out.rearrange("i c (s h) w -> i s c (h w)", s=2)

            def half(a, image, j):
                return a[bass.ds(image + j // 2, 1), j % 2, :, :].rearrange("a c n -> c (a n)")

            def load(src, image, j):
                sp.dma_start(xbuf[:, j, :], half(src, image, j)).then_inc(x_in[j], 16)

            def store(image, j):
                sp.dma_start(half(o_half, image, j), xbuf[:, j, :]).then_inc(t_out[j], 16)

            def attention(g, bodies):
                def body(b, last):
                    for j in range(XB):
                        image = g * GSIZE + b * (XB // 2)
                        done(sp, "t_placed", g * GQ + b * BODY + (2 * j + 1))
                        store(image, j)
                        sp.wait_ge(t_out[j], (g * (2 * BODIES) + b) * 16 + 16)
                        sp.sem_inc(waited, 1)
                        if not last:
                            load(x_half, image + XB // 2, j)
                for j in range(XB):
                    load(x_half, g * GSIZE, j)
                if bodies > 1:
                    with sp.Fori(0, bodies - 1) as b:
                        body(b, False)
                body(bodies - 1, True)

            with sp.Fori(0, GROUPS) as g:
                attention(g, BODIES)
                for j in range(XB):
                    load(o_half, g * GSIZE, j)

                def finish(b, last):
                    for j in range(XB):
                        sp.wait_ge(c_half, g * (2 * GSIZE) + b * XB + (j + 1))
                        store(g * GSIZE + b * (XB // 2), j)
                        sp.wait_ge(t_out[j], (g * (2 * BODIES) + b) * 16 + (BODIES + 1) * 16)
                        sp.sem_inc(waited, 1)
                        if not last:
                            load(o_half, g * GSIZE + (b + 1) * (XB // 2), j)
                with sp.Fori(0, BODIES - 1) as b:
                    finish(b, False)
                finish(BODIES - 1, True)
            attention(GROUPS, 1)

        @block.gpsimd
        def _(pool):
            nc.gpsimd.memset(halfpow[:, :], -0.5).then_inc(pool_set, 1)
            nc.gpsimd.memset(xnT[:, :, :, C:C + 1], 1.0).then_inc(pool_set, 1)
            nc.gpsimd.memset(nT[:, :, :, C:C + 2], 1.0).then_inc(pool_set, 1)
            nc.gpsimd.memset(w1T[:, :], 0.0).then_inc(pool_set, 1)
            nc.gpsimd.memset(w2T[:, :, :], 0.0).then_inc(pool_set, 1)
            nc.gpsimd.memset(gam[:, :, :], 0.0).then_inc(pool_set, 1)
            pool.wait_ge(pool_set, POOL_SETS)

            def met():
                pool.sem_inc(waited, 1)

            def moments(s, eps):
                def step(k, q, place, use, last):
                    b = k % 2
                    a, w = st[s][:, b, :, :], mo[s][:, b, :, :]
                    done(pool, s + "_stats", q)
                    done(pool, s + "_norm", q - 2)
                    nc.gpsimd.tensor_tensor(w[:, 0, :], a[:, :, 1], a[:, :, 4], ALU.add).then_inc(S[s + "_sum"], 1)
                    nc.gpsimd.tensor_tensor(w[:, 1, :], a[:, :, 1], a[:, :, 4], ALU.subtract).then_inc(S[s + "_dif"], 1)
                    nc.gpsimd.tensor_tensor(w[:, 2, :], a[:, :, 2], a[:, :, 5], ALU.add).then_inc(S[s + "_m2"], 1)
                    done(pool, s + "_sum", q)
                    done(pool, s + "_dif", q)
                    met()
                    nc.gpsimd.tensor_scalar(w[:, 3:5, :], w[:, 0:2, :], -0.5, 0.0, ALU.mult, ALU.add)\
                        .then_inc(S[s + "_half"], 1)
                    done(pool, s + "_m2", q)
                    met()
                    nc.gpsimd.tensor_scalar(w[:, 6, :], w[:, 2, :], 1.0 / C, eps, ALU.mult, ALU.add).then_inc(S[s + "_v"], 1)
                    done(pool, s + "_half", q)
                    nc.gpsimd.tensor_tensor(w[:, 5, :], w[:, 4, :], w[:, 4, :], ALU.mult).then_inc(S[s + "_d2"], 1)
                    done(pool, s + "_d2", q)
                    done(pool, s + "_v", q)
                    nc.gpsimd.tensor_tensor(w[:, 7, :], w[:, 5, :], w[:, 6, :], ALU.add).then_inc(S[s + "_var"], 1)
                    done(pool, s + "_var", q)
                    nc.gpsimd.tensor_tensor(w[:, 8, :], w[:, 7, :], halfpow[0:TN, 0:T], ALU.pow).then_inc(S[s + "_rstd"], 1)
                    done(pool, s + "_rstd", q)
                    nc.gpsimd.tensor_tensor(w[:, 9, :], w[:, 3, :], w[:, 8, :], ALU.mult).then_inc(S[s + "_shift"], 1)
                return step

            def center_squares(k, q, place, use, last):
                b = k % 2
                done(pool, "cen_bd", q)
                done(pool, "q_ps", q - 2)
                v = cbd[:, b, :, :, :].rearrange("c k h m -> c (k h m)")
                nc.gpsimd.tensor_tensor(csq[:, b, :], v, v, ALU.mult).then_inc(S["cen_sq"], 1)

            def inverse_norms(k, q, place, use, last):
                done(pool, "n2_done", q)
                met()
                nc.gpsimd.tensor_scalar(n2c[:, :], n2[:, :], NORM_FLOOR, 0.0, ALU.max, ALU.add).then_inc(S["n2_floor"], 1)
                done(pool, "n2_floor", q)
                done(pool, "cos_done", q - 1)
                met()
                i32 = mybir.dt.int32
                nc.gpsimd.tensor_scalar(ninv[:, :].bitcast(i32), n2c[:, :].bitcast(i32), -0.5, float(0x5F3759DF),
                                        ALU.mult, ALU.add).then_inc(S["n_guess"], 1)
                before = "n_guess"
                for i in range(3):
                    done(pool, before, q)
                    nc.gpsimd.tensor_tensor(ny2[:, :], ninv[:, :], ninv[:, :], ALU.mult).then_inc(S[f"n_square{i}"], 1)
                    done(pool, f"n_square{i}", q)
                    nc.gpsimd.tensor_tensor(nxy[:, :], ny2[:, :], n2c[:, :], ALU.mult).then_inc(S[f"n_part{i}"], 1)
                    done(pool, f"n_part{i}", q)
                    met()
                    nc.gpsimd.tensor_scalar(nxy[:, :], nxy[:, :], -0.5, 1.5, ALU.mult, ALU.add)\
                        .then_inc(S[f"n_factor{i}"], 1)
                    done(pool, f"n_factor{i}", q)
                    nc.gpsimd.tensor_tensor(ninv[:, :], ninv[:, :], nxy[:, :], ALU.mult).then_inc(S[f"n_newton{i}"], 1)
                    before = f"n_newton{i}"

            def center_norms(k, q, place, use, last):
                b = k % 2
                done(pool, "cen_n2", q)
                done(pool, "q_done", q - 2)
                nc.gpsimd.tensor_tensor(cinv[:, b:b + 1], cn2[:, b:b + 1], halfpow[0:HM, 0:1], ALU.pow).then_inc(S["cen_inv"], 1)

            def over_partitions(n, i):
                pool.wait_ge(g_max, n)
                met()
                nc.gpsimd.partition_all_reduce(gam[:, i, 1:2], gam[:, i, 0:1], 128, MAX).then_inc(g_all, 1)

            def gather(k, q, place, use, last):
                if k % 2 == 0:
                    pool.wait_ge(x_in[k // 2], use * 16 + 16)
                done(pool, "x_T", q - 2)
                met()
                nc.gpsimd.tensor_copy(xq[:, k % 2, :].rearrange("c (r w) -> c r w", w=QS), image_rows(k))\
                    .then_inc(S["x_side"], 1)

            def place_t(k, q, place, use, last):
                done(pool, "t_done", q)
                met()
                nc.gpsimd.tensor_copy(image_rows(k), tq[:, k % 2, :].rearrange("c (r w) -> c r w", w=QS))\
                    .then_inc(S["t_placed"], 1)

            attention = [(0, gather), (1, moments("x", EPS_C)), (2, inverse_norms), (4, place_t), (1, center_squares),
                         (1, center_norms), (3, moments("t", EPS_T), FFN)]
            with pool.Fori(0, GROUPS) as g:
                pipeline(pool, g, attention, BODIES)
                over_partitions(2 * g + 1, 0)
                over_partitions(2 * g + 2, 1)
            pipeline(pool, GROUPS, attention, 1, ffn=False)

        @block.scalar
        def _(act):
            def normalise(s, b0):
                def step(k, q, place, use, last):
                    done(act, s + "_shift", q)
                    if s == "x":
                        done(act, "u_ps", q - 4)
                    else:
                        done(act, "n_ps", q - 2)
                    m = mo[s][:, k % 2, :, :]
                    for t in range(T):
                        src = bank(b0, TN, C, t * C) if t < TA else bank(b0 + 1, TN, C, (t - TA) * C)
                        dst = xnT[:, k % 4, t, 0:C] if s == "x" else nT[:, k % 2, t, 0:C]
                        ins = nc.scalar.activation(dst, src, ACT.Identity, bias=m[:, 9, t:t + 1], scale=m[:, 8, t:t + 1])
                    ins.then_inc(S[s + "_norm"], 1)
                return step

            def copy_x(k, q, place, use, last):
                done(act, "xn_ps", q)
                done(act, "s_ps", q - 2)
                nc.scalar.copy(xn[:, k % 2, 0:NA], bank(0, C + 1, NA))
                nc.scalar.copy(xn[:, k % 2, NA:QN], bank(1, C + 1, NB)).then_inc(S["xn_copied"], 1)

            def squares(t0, t1):
                def step(k, q, place, use, last):
                    if t0 == 0:
                        done(act, "n2_done", q - 1)
                    for t in range(t0, t1):
                        act.wait_ge(f_ps, q * T + (START + t + 1))
                        nc.scalar.activation(sq[:, t, :], bank(2 + t % 2, TN, D), ACT.Square).then_inc(f_sq, 1)
                return step

            def sigmoid(k, q, place, use, last):
                done(act, "cos_done", q)
                done(act, "sim_done", q - 2)
                nc.scalar.activation(sig[:, k % 2, :], cosb[:, :], ACT.Sigmoid, bias=betac[:, :]).then_inc(S["sig_done"], 1)

            def copy_eq(k, q, place, use, last):
                done(act, "eqT_ps", q)
                done(act, "first_ps", q - 1)
                nc.scalar.copy(eqT[:, :], ps[:, 4, :].bitcast(bf16)[:, 0:QN]).then_inc(S["eqT_copied"], 1)

            def copy_sim(k, q, place, use, last):
                done(act, "simT_ps", q)
                done(act, "o_ps", q - 1)
                nc.scalar.copy(simT[:, 0:NA], bank(4, HM, NA))
                nc.scalar.copy(simT[:, NA:QN], bank(5, HM, NB)).then_inc(S["simT_copied"], 1)

            def n_high():
                def step(k, q, place, use, last):
                    done(act, "n_ps", q)
                    o = tok[:, bass.ds(place, 1), 0, :].rearrange("p a n -> p (a n)")
                    nc.scalar.copy(o[:, 0:NA], bank(6, C + 2, NA))
                    nc.scalar.copy(o[:, NA:QN], bank(7, C + 2, NB)).then_inc(S["n_hi"], 1)
                return step

            def attention():
                return [(4, normalise("t", 6), FFN), (2, squares(5, 7)), (3, copy_sim), (4, n_high(), FFN),
                        (1, normalise("x", 0)), (1, copy_x), (2, sigmoid), (1, squares(0, 4)), (2, copy_eq),
                        (1, squares(4, 5))]

            act.wait_ge(w_loaded, 16 * LOADS)
            with act.Fori(0, GROUPS) as g:
                pipeline(act, g, attention(), BODIES)
                tile0 = g * (2 * GQ)

                def gelu(i, s):
                    act.wait_ge(bh_ps, i + (START + 1))
                    act.wait_ge(b_lo, i + (START - 1))
                    nc.scalar.activation(gel[:, s, :].rearrange("p (c n) -> p c n", c=FC), ps[:, 3 * s:3 * s + 3, 0:HT],
                                         ACT.Gelu, scale=scale[:, 0:1]).then_inc(b_gelu, 1)

                def y_out(i, place, s):
                    act.wait_ge(by_ps, i + (START + 1))
                    o = y32[0:C, bass.ds(place, 1), s * HT:(s + 1) * HT].rearrange("c a n -> c (a n)")
                    nc.scalar.activation(o, bank(6 + s, C, HT), ACT.Identity, bias=b2c[:, :]).then_inc(b_y, 1)

                act.wait_ge(g_scale, 2 * g + 1)
                gelu(tile0, 0)
                with act.Fori(0, GQ - 1) as p:
                    i = tile0 + 2 * p
                    gelu(i + 1, 1)
                    y_out(i, p, 0)
                    gelu(i + 2, 0)
                    y_out(i + 1, p, 1)
                i = tile0 + (2 * GQ - 2)
                gelu(i + 1, 1)
                y_out(i, GQ - 1, 0)
                y_out(i + 1, GQ - 1, 1)
            pipeline(act, GROUPS, attention(), 1, ffn=False)

        @block.vector
        def _(dve):
            count = [0]

            def step(ins):
                count[0] += 1
                ins.then_inc(dve_set, 1)
                dve.wait_ge(dve_set, count[0])

            v = nc.vector
            dve.wait_ge(w_loaded, 16 * LOADS)
            dve.wait_ge(pool_set, POOL_SETS)
            step(v.tensor_copy(ident16[:, :], ident))
            step(v.tensor_copy(first16[:, :], const("first")))
            for w, gt, total, mean, n in ((w1, gt1, wsum1, wmean1, G1 * C), (w2, gt2, wsum2, wmean2, G2 * F)):
                step(v.reduce_sum(total[:, :], w[:, :, :], AX.X))
            assert count[0] == DVE_SUMS
            dve.wait_ge(pe_set, 1)
            step(v.tensor_scalar(wmean1[:, :], bank(0, G1, GROUPS), 1.0 / (G1 * C), None, ALU.mult))
            step(v.tensor_scalar(wmean2[:, :], bank(1, G2, GROUPS), 1.0 / (G2 * F), None, ALU.mult))
            for w, gt, mean, rows, n in ((w1, gt1, wmean1, G1, C), (w2, gt2, wmean2, G2, F)):
                m = mean[:, :].unsqueeze(2).broadcast_to([rows, GROUPS, n])
                step(v.tensor_tensor(gt[:, :, :], w[:, :, :], m, ALU.is_gt))
                step(v.tensor_tensor(w[:, :, :], w[:, :, :], m, ALU.is_lt))
                step(v.tensor_tensor(w[:, :, :], gt[:, :, :], w[:, :, :], ALU.subtract))
            step(v.tensor_copy(wfT[:, :], bank(2, C + 1, D)))
            wpT = bank(3, C, D).rearrange("r (k o) -> r k o", k=4)
            for h in range(2):
                step(v.tensor_scalar(wph[:, :, h, :], wpT, const("head_of_row", C)[:, h:h + 1], None, ALU.mult))
            step(v.tensor_copy(V[:, :, 2 * C:VN], const("last_row", C + 1).unsqueeze(1).broadcast_to([C + 1, 4, 2])))
            r, m = slice(C, C + 2), const("bias_part")
            step(v.tensor_copy(b1h[r, :], b1s[r, :]))
            step(v.tensor_tensor(b1l[r, :], b1s[r, :], b1h[r, :], ALU.subtract))
            step(v.tensor_scalar(b1l[r, :], b1l[r, :], m[r, 1:2], None, ALU.mult))
            step(v.scalar_tensor_tensor(w1T[r, :], b1h[r, :], m[r, 0:1], b1l[r, :], ALU.mult, ALU.add))
            assert count[0] == DVE_SIGNS
            dve.wait_ge(pe_set, 2)
            for i in range(2):
                step(v.tensor_copy(V[:, 2 * i:2 * i + 2, 0:2 * C],
                                   bank(4 + i, C + 1, 4 * C).rearrange("c (k o) -> c k o", k=2)))
            step(v.tensor_copy(w1T[0:C, 0:G1 * GROUPS], bank(6, C, G1 * GROUPS)))
            step(v.tensor_copy(w2T[:, :, 0:G2 * GROUPS],
                               bank(7, 128, FC * C).rearrange("f (c o) -> f c o", c=FC)[:, :, 0:G2 * GROUPS]))
            assert count[0] == DVE_ALL

            def stats(s, b0):
                def step(k, q, place, use, last):
                    done(dve, s + "_T", q)
                    done(dve, s + "_rstd", q - 2)
                    for t in range(T):
                        src = bank(b0, TN, C, t * C) if t < TA else bank(b0 + 1, TN, C, (t - TA) * C)
                        last_one = v.bn_stats(st[s][:, k % 2, t, :], src)
                    last_one.then_inc(S[s + "_stats"], 1)
                return step

            def pooled(k, q, place, use, last):
                done(dve, "xn_ps", q)
                done(dve, "xn_copied", q)
                done(dve, "u_done", q - 4)
                v.tensor_scalar(cenx[:, k % 4, :], bank(1, C + 1, CENTERS, NB), 1.0 / (PW * PW), None, ALU.mult)\
                    .then_inc(S["cen_x"], 1)

            def centers(k, q, place, use, last):
                done(dve, "cen_f", q)
                done(dve, "q_ps", q - 2)
                f = bank(0, C, 4 * CENTERS).rearrange("r (k m) -> r k m", k=4)
                mask = const("head_of_row", C)
                v.tensor_tensor(cbd[:, k % 2, :, :, :], f.unsqueeze(2).broadcast_to([C, 4, 2, CENTERS]),
                                mask.unsqueeze(1).unsqueeze(3).broadcast_to([C, 4, 2, CENTERS]), ALU.mult)\
                    .then_inc(S["cen_bd"], 1)

            def center_floor(k, q, place, use, last):
                done(dve, "q_ps", q)
                done(dve, "cen_inv", q - 2)
                v.tensor_scalar(cn2[:, k % 2:k % 2 + 1], bank(0, HM, 1, 64), NORM_FLOOR, None, ALU.max)\
                    .then_inc(S["cen_n2"], 1)

            def q_scaled(k, q, place, use, last):
                done(dve, "cen_inv", q)
                v.tensor_scalar(qT[:, :], bank(0, HM, C + 1, 128), cinv[:, k % 2:k % 2 + 1], alphac[:, :],
                                ALU.mult, ALU.mult).then_inc(S["q_scaled"], 1)

            def q_placed(k, q, place, use, last):
                done(dve, "q_T", q)
                done(dve, "s_ps", q - 2)
                v.tensor_copy(Q[:, k % 2, :], bank(0, C + 1, HM, 256)).then_inc(S["q_done"], 1)

            def norms(k, q, place, use, last):
                done(dve, "n2_floor", q - 1)
                for t0, t1 in ((0, TA), (TA, T)):
                    dve.wait_ge(f_sq, q * T + (START + t1))
                    ins = v.reduce_sum(n2[:, t0 * HEADS:t1 * HEADS],
                                       sq[:, t0:t1, :].rearrange("p t (h d) -> p (t h) d", d=HD), AX.X)
                ins.then_inc(S["n2_done"], 1)

            def heads(ap):
                return ap.rearrange("p (h m) -> p h m", m=CENTERS)

            def over_centers(ap):
                return ap.unsqueeze(2).broadcast_to([TN, T * HEADS, CENTERS])

            def cosine(k, q, place, use, last):
                done(dve, "s_ps", q)
                done(dve, "n_newton2", q)
                done(dve, "sig_done", q - 1)
                v.tensor_tensor(heads(cosb[:, :]), heads(pair(2, TN, T * HM)), over_centers(ninv[:, :]), ALU.mult)\
                    .then_inc(S["cos_done"], 1)

            def maxima(k, q, place, use, last):
                done(dve, "sig_done", q)
                v.tensor_reduce(top[:, :], heads(sig[:, k % 2, :]), AX.X, ALU.max).then_inc(S["top_done"], 1)

            def marks(k, q, place, use, last):
                done(dve, "top_done", q)
                done(dve, "eqT_ps", q - 1)
                v.tensor_tensor(heads(eq[:, :]), heads(sig[:, k % 2, :]), over_centers(top[:, :]), ALU.is_equal)\
                    .then_inc(S["eq_done"], 1)

            def masked(k, q, place, use, last):
                done(dve, "first_ps", q)
                done(dve, "u_ps", q - 2)
                v.scalar_tensor_tensor(sim[:, k % 2, :], pair(4, TN, T * HM), -1.0, sig[:, k % 2, :],
                                       ALU.is_equal, ALU.mult).then_inc(S["sim_done"], 1)

            def summed(k, q, place, use, last):
                done(dve, "u_ps", q)
                done(dve, "a_ps", q - 1)
                v.tensor_tensor(heads(uT[:, :]), heads(bank(4, C + 1, HM)),
                                cenx[:, k % 4, :].unsqueeze(1).broadcast_to([C + 1, HEADS, CENTERS]), ALU.add)\
                    .then_inc(S["u_done"], 1)

            def aggregated(k, q, place, use, last):
                done(dve, "a_ps", q)
                v.reciprocal(rden[:, :], bank(5, HM, 1, 2 * C)).then_inc(S["a_rden"], 1)
                done(dve, "a_rden", q)
                v.tensor_scalar(hmul[:, :], const("head_of_center"), rden[:, :], None, ALU.mult).then_inc(S["a_mul"], 1)
                done(dve, "a_mul", q)
                v.tensor_scalar(a1[:, :], bank(5, HM, C), hmul[:, 0:1], None, ALU.mult).then_inc(S["a_half"], 1)
                done(dve, "a_half", q)
                done(dve, "o_ps", q - 1)
                v.scalar_tensor_tensor(aggp[:, :], bank(5, HM, C, C), hmul[:, 1:2], a1[:, :], ALU.mult, ALU.add)\
                    .then_inc(S["a_done"], 1)

            def residual(k, q, place, use, last):
                done(dve, "o_ps", q)
                if with_ffn[0]:
                    done(dve, "t_T", q - 2)
                done(dve, "t_placed", q - 2)
                for b, lo, n in ((4, 0, NA // QS), (5, NA // QS, NB // QS)):
                    o = bank(b, C, n * QS).rearrange("c (r w) -> c r w", w=QS)
                    t = tq[:, k % 2, lo * QS:(lo + n) * QS].rearrange("c (r w) -> c r w", w=QS)
                    ins = v.scalar_tensor_tensor(t, o, bpc[:, :], image_rows(k, lo, n), ALU.add, ALU.add)
                ins.then_inc(S["t_done"], 1)

            def n_low():
                def step(k, q, place, use, last):
                    done(dve, "n_hi", q)
                    hi, lo = (tok[:, bass.ds(place, 1), i, :].rearrange("p a n -> p (a n)") for i in range(2))
                    v.tensor_tensor(lo[:, 0:NA], bank(6, C + 2, NA), hi[:, 0:NA], ALU.subtract)
                    v.tensor_tensor(lo[:, NA:QN], bank(7, C + 2, NB), hi[:, NA:QN], ALU.subtract).then_inc(S["n_lo"], 1)
                return step

            def h_largest(u0, u1):
                def step(k, q, place, use, last):
                    for u in range(u0, u1):
                        dve.wait_ge(h_ps, q * (2 * FC) + (START + u + 1))
                        o = hmax[:, bass.ds(place * (2 * FC) + u, 1)]
                        v.tensor_reduce(o, bank(6 + u % 2, 128, HT), AX.X, ALU.max, apply_absolute_value=True)\
                            .then_inc(h_max, 1)
                return step

            with_ffn = [True]

            def attention():
                return [(1, stats("x", 0)), (2, norms), (4, n_low(), FFN), (3, summed), (4, h_largest(0, 2), FFN),
                        (3, aggregated), (4, h_largest(2, 3), FFN), (2, cosine), (4, h_largest(3, 4), FFN), (1, pooled),
                        (3, residual), (4, h_largest(4, 6), FFN), (1, centers), (2, maxima), (3, stats("t", 6), FFN),
                        (1, center_floor), (2, marks), (1, q_scaled), (1, q_placed), (2, masked)]

            def largest(src, n, i, rows):
                v.tensor_reduce(gam[0:rows, i, 0:1], src, AX.X, ALU.max).then_inc(g_max, 1)
                dve.wait_ge(g_all, n)
                v.tensor_scalar(den[:, i, 0:1], gam[:, i, 1:2], EPS_Q, None, ALU.add).then_inc(g_eps, 1)
                dve.wait_ge(g_eps, n)
                v.reciprocal(den[:, i, 1:2], den[:, i, 0:1]).then_inc(g_rec, 1)
                dve.wait_ge(g_rec, n)
                v.tensor_scalar(scale[:, i:i + 1], den[:, i, 1:2], QB, None, ALU.mult).then_inc(g_scale, 1)
                dve.wait_ge(g_scale, n)
                dve.sem_inc(waited, 1)

            with dve.Fori(0, GROUPS) as g:
                pipeline(dve, g, attention(), BODIES)
                dve.wait_ge(h_max, g * (GQ * 2 * FC) + (START + GQ * 2 * FC))
                largest(hmax[:, :], 2 * g + 1, 0, 128)
                tile0 = g * (2 * GQ)

                def split(i, s):
                    dve.wait_ge(b_gelu, i + (START + 1))
                    dve.wait_ge(by_ps, i + (START - 1))
                    v.tensor_scalar(ghi[:, s, :], gel[:, s, :], QCLIP, None, ALU.min).then_inc(b_hi, 1)
                    dve.wait_ge(b_hi, i + (START + 1))
                    v.scalar_tensor_tensor(glo[:, s, :], gel[:, s, :], QCLIP, ghi[:, s, :], ALU.min, ALU.subtract)\
                        .then_inc(b_lo, 1)

                def y_largest(i, place, s):
                    dve.wait_ge(b_y, i + (START + 1))
                    y = y32[0:C, bass.ds(place, 1), s * HT:(s + 1) * HT].rearrange("c a n -> c (a n)")
                    v.tensor_reduce(ymax[:, bass.ds(2 * place + s, 1)], y, AX.X, ALU.max, apply_absolute_value=True)\
                        .then_inc(b_ymax, 1)

                split(tile0, 0)
                with dve.Fori(0, GQ - 1) as p:
                    i = tile0 + 2 * p
                    split(i + 1, 1)
                    y_largest(i, p, 0)
                    split(i + 2, 0)
                    y_largest(i + 1, p, 1)
                i = tile0 + (2 * GQ - 2)
                split(i + 1, 1)
                y_largest(i, GQ - 1, 0)
                y_largest(i + 1, GQ - 1, 1)
                dve.wait_ge(b_ymax, g * (2 * GQ) + (START + 2 * GQ))
                largest(ymax[:, :], 2 * g + 2, 1, C)

                with dve.Fori(0, BODIES) as b:
                    for k in range(BODY):
                        q = g * GQ + b * BODY + k
                        if k % 2 == 0:
                            dve.wait_ge(x_in[k // 2], (g * (2 * BODIES) + b) * 16 + (BODIES + 1) * 16)
                        y = y32[0:C, bass.ds(b * BODY + k, 1), :].rearrange("c a n -> c (a n)")
                        v.tensor_scalar(y, y, scale[0:C, 1:2], QCLIP, ALU.mult, ALU.min).then_inc(S["c_min"], 1)
                        done(dve, "c_min", q)
                        ins = v.scalar_tensor_tensor(image_rows(k), y.rearrange("c (r w) -> c r w", w=QS), -QCLIP,
                                                     image_rows(k), ALU.max, ALU.add)
                        if k % 2 == 1:
                            ins.then_inc(c_half, 1)
            with_ffn[0] = False
            pipeline(dve, GROUPS, attention(), 1, ffn=False)

        @block.tensor
        def _(pe):
            mm, tr = nc.tensor.matmul, nc.tensor.transpose
            pe.wait_ge(w_loaded, 16 * LOADS)
            pe.wait_ge(dve_set, DVE_SUMS)
            mm(bank(0, G1, GROUPS), ones[0:G1, 0:G1], wsum1[:, :], start=True, stop=True)
            mm(bank(1, G2, GROUPS), ones[0:G2, 0:G2], wsum2[:, :], start=True, stop=True)
            for k in range(4):
                tr(bank(2, C + 1, C, k * C), wf[:, k, :], ident[0:C, 0:C])
                ins = tr(bank(3, C, C, k * C), wp[:, k * C:(k + 1) * C], ident[0:C, 0:C])
            ins.then_inc(pe_set, 1)
            pe.wait_ge(dve_set, DVE_SIGNS)
            for k in range(4):
                mm(bank(4 + k // 2, C + 1, 2 * C, k % 2 * 2 * C), wv[:, k, :],
                   wph[:, k, :, :].rearrange("r h o -> r (h o)"), start=True, stop=True)
            for g in range(GROUPS):
                tr(bank(6, C, G1, g * G1), w1[:, g, :], ident[0:G1, 0:G1])
                for c in range(FC):
                    ins = tr(bank(7, 128, G2, c * C + g * G2), w2[:, g, c * 128:(c + 1) * 128], ident[0:G2, 0:G2])
            ins.then_inc(pe_set, 1)
            pe.wait_ge(dve_set, DVE_ALL)

            def tile_bank(b0, rows, n, t):
                return bank(b0, rows, n, t * n) if t < TA else bank(b0 + 1, rows, n, (t - TA) * n)

            def to_tokens(s, b0):
                def step(k, q, place, use, last):
                    if s == "x":
                        done(pe, "x_side", q)
                        done(pe, "q_done", q - 1)
                    else:
                        done(pe, "t_done", q)
                        pe.wait_ge(h_max, q * (2 * FC) + START)
                    for t in range(T):
                        src = (xq if s == "x" else tq)[:, k % 2, t * TN:(t + 1) * TN]
                        ins = tr(tile_bank(b0, TN, C, t), src, ident[0:C, 0:C])
                    ins.then_inc(S[s + "_T"], 1)
                return step

            def x_back(k, q, place, use, last):
                done(pe, "x_norm", q)
                for t in range(T):
                    mm(bank(1, C + 1, CENTERS, NB), xnT[:, k % 4, t, :], poolm[:, t, :], start=t == 0, stop=t == T - 1)
                for t in range(T):
                    ins = tr(tile_bank(0, C + 1, TN, t), xnT[:, k % 4, t, :], ident[0:TN, 0:TN])
                ins.then_inc(S["xn_ps"], 1)

            def centers(k, q, place, use, last):
                done(pe, "cen_x", q)
                done(pe, "xn_copied", q)
                for c in range(4):
                    ins = mm(bank(0, C, CENTERS, c * CENTERS), wfT[:, c * C:(c + 1) * C], cenx[:, k % 4, :],
                             start=True, stop=True)
                ins.then_inc(S["cen_f"], 1)

            def center_products(k, q, place, use, last):
                done(pe, "cen_bd", q)
                done(pe, "cen_sq", q)
                mm(bank(0, HM, 1, 64), csq[:, k % 2, :], ones[0:C, 0:1], start=True, stop=True)
                n = 2 * CENTERS
                for c in range(4):
                    ins = mm(ps[c * n:(c + 1) * n, 0, 128:128 + C + 1],
                             cbd[:, k % 2, c, :, :].rearrange("r h m -> r (h m)"), wf[:, c, :], start=True, stop=True)
                ins.then_inc(S["q_ps"], 1)

            def q_back(k, q, place, use, last):
                done(pe, "q_scaled", q)
                tr(bank(0, C + 1, HM, 256), qT[:, :], ident).then_inc(S["q_T"], 1)

            def features(t0, t1):
                def step(k, q, place, use, last):
                    if t0 == 0:
                        done(pe, "xn_copied", q)
                        done(pe, "cos_done", q - 1)
                    for t in range(t0, t1):
                        if t >= 2:
                            pe.wait_ge(f_sq, q * T + (START + t - 1))
                        mm(bank(2 + t % 2, TN, D), xn[:, k % 2, t * TN:(t + 1) * TN], wfT[:, :], start=True, stop=True)\
                            .then_inc(f_ps, 1)
                return step

            def scores(k, q, place, use, last):
                pe.wait_ge(f_sq, q * T + (START + T))
                done(pe, "q_done", q)
                for t in range(T):
                    ins = mm(tile_bank(2, TN, HM, t), xn[:, k % 2, t * TN:(t + 1) * TN], Q[:, k % 2, :],
                             start=True, stop=True)
                ins.then_inc(S["s_ps"], 1)

            def marks_back(k, q, place, use, last):
                done(pe, "eq_done", q)
                done(pe, "t_done", q - 1)
                o = ps[:, 4, :].bitcast(bf16)
                for t in range(T):
                    ins = tr(o[:, t * TN:(t + 1) * TN], eq[:, t * HM:(t + 1) * HM], ident16[0:TN, 0:TN])
                ins.then_inc(S["eqT_ps"], 1)

            def find_first(k, q, place, use, last):
                done(pe, "eqT_copied", q)
                for t in range(T):
                    ins = mm(tile_bank(4, TN, HM, t), eqT[:, t * TN:(t + 1) * TN], first16[:, :], start=True, stop=True)
                ins.then_inc(S["first_ps"], 1)

            def sim_back(k, q, place, use, last):
                done(pe, "sim_done", q)
                for t in range(T):
                    ins = tr(tile_bank(4, HM, TN, t), sim[:, k % 2, t * HM:(t + 1) * HM], ident[0:TN, 0:TN])
                ins.then_inc(S["simT_ps"], 1)

            def aggregate(k, q, place, use, last):
                done(pe, "simT_copied", q)
                for t in range(T):
                    ins = mm(bank(4, C + 1, HM), xnT[:, k % 4, t, :], sim[:, k % 2, t * HM:(t + 1) * HM],
                             start=t == 0, stop=t == T - 1)
                ins.then_inc(S["u_ps"], 1)

            def project(k, q, place, use, last):
                done(pe, "u_done", q)
                for c in range(4):
                    n = 2 * CENTERS
                    ins = mm(ps[c * n:(c + 1) * n, 5, 0:VN], uT[:, c * n:(c + 1) * n], V[:, c, :], start=True, stop=True)
                ins.then_inc(S["a_ps"], 1)

            def spread(k, q, place, use, last):
                done(pe, "a_done", q)
                mm(bank(4, C, NA), aggp[:, :], simT[:, 0:NA], start=True, stop=True)
                mm(bank(5, C, NB), aggp[:, :], simT[:, NA:QN], start=True, stop=True).then_inc(S["o_ps"], 1)

            def t_back(k, q, place, use, last):
                done(pe, "t_norm", q)
                for t in range(T):
                    ins = tr(tile_bank(6, C + 2, TN, t), nT[:, k % 2, t, :], ident[0:TN, 0:TN])
                ins.then_inc(S["n_ps"], 1)

            def hidden(dst, place, s, c):
                for part in range(2):
                    ins = mm(dst, w1T[:, c * 128:(c + 1) * 128],
                             tok[:, bass.ds(place, 1), part, s * HT:(s + 1) * HT].rearrange("p a n -> p (a n)"),
                             start=part == 0, stop=part == 1)
                return ins

            def hidden_tiles(u0, u1):
                def step(k, q, place, use, last):
                    if u0 == 0:
                        done(pe, "n_lo", q)
                    for u in range(u0, u1):
                        if u >= 2:
                            pe.wait_ge(h_max, q * (2 * FC) + (START + u - 1))
                        hidden(bank(6 + u % 2, 128, HT), place, u // FC, u % FC).then_inc(h_ps, 1)
                return step

            def attention():
                return [(2, features(6, 7)), (3, sim_back), (4, t_back, FFN), (2, scores), (3, aggregate),
                        (4, hidden_tiles(0, 2), FFN), (3, project), (4, hidden_tiles(2, 4), FFN), (1, x_back), (3, spread),
                        (4, hidden_tiles(4, 5), FFN), (1, centers), (4, hidden_tiles(5, 6), FFN), (1, features(0, 2)),
                        (3, to_tokens("t", 6), FFN), (1, center_products), (1, features(2, 5)), (2, marks_back),
                        (1, q_back), (1, features(5, 6)), (2, find_first), (0, to_tokens("x", 0))]

            with pe.Fori(0, GROUPS) as g:
                pipeline(pe, g, attention(), BODIES)
                tile0 = g * (2 * GQ)

                def up(i, place, s):
                    pe.wait_ge(b_gelu, i + (START - 1))
                    for c in range(FC):
                        ins = hidden(bank(3 * s + c, 128, HT), place, s, c)
                    ins.then_inc(bh_ps, 1)

                def down(i, s):
                    pe.wait_ge(b_lo, i + (START + 1))
                    pe.wait_ge(b_y, i + (START - 1))
                    for n, (part, c) in enumerate((part, c) for part in (ghi, glo) for c in range(FC)):
                        ins = mm(bank(6 + s, C, HT), w2T[:, c, :], part[:, s, c * HT:(c + 1) * HT],
                                 start=n == 0, stop=n == 2 * FC - 1)
                    ins.then_inc(by_ps, 1)

                pe.wait_ge(h_max, g * (GQ * 2 * FC) + (START + GQ * 2 * FC))
                up(tile0, 0, 0)
                with pe.Fori(0, GQ - 1) as p:
                    i = tile0 + 2 * p
                    up(i + 1, p, 1)
                    down(i, 0)
                    up(i + 2, p + 1, 0)
                    down(i + 1, 1)
                i = tile0 + (2 * GQ - 2)
                up(i + 1, GQ - 1, 1)
                down(i, 0)
                down(i + 1, 1)
            pipeline(pe, GROUPS, attention(), 1, ffn=False)


INPUTS = ["x"] + ["L0_conv_" + n for n in ("Wf", "bf", "Wv", "bv", "Wp", "bp", "sim_alpha", "sim_beta")] \
    + ["L0_ffn_" + n for n in ("W1", "b1", "W2", "b2")]


def kernel(**inputs):
    import concourse.bacc as bacc
    from concourse.bass_utils import run_bass_kernel_spmd

    nc = bacc.Bacc("TRN2", target_bir_lowering=False, num_devices=1)
    arrays = {f"in_{n}": np.ascontiguousarray(inputs[n]) for n in INPUTS}
    arrays["in_constants"] = SHAPE_CONSTANTS
    args = [nc.dram_tensor(n, a.shape, mybir.dt.from_np(a.dtype), kind="ExternalInput").ap() for n, a in arrays.items()]
    args.append(nc.dram_tensor("out_0", (IMAGES, C, SIDE, SIDE), mybir.dt.float32, kind="ExternalOutput").ap())
    build(nc, *args)
    r = run_bass_kernel_spmd(nc, [arrays], core_ids=[0])
    return r.results[0]["out_0"]
```

```python
import numpy as np
import concourse.bass as bass
from concourse import mybir
from contextlib import ExitStack

IMAGES, C, SIDE = 32, 96, 56
PIX = SIDE * SIDE
QS = SIDE // 2
QN = QS * QS
HEADS, HD, CENTERS = 8, 48, 16
D = HEADS * HD
HM = HEADS * CENTERS
ROWS_T = 4
T = QS // ROWS_T
TN = ROWS_T * QS
PW = QS // 4
BN = TN + CENTERS
HALF = PIX // 2
TA = 4
NA, NB = TA * TN, (T - TA) * TN
GROUPS, GSIZE = 5, IMAGES // 5
GQ = GSIZE * 4
XB = 4
BODY = 2 * XB
BODIES = GQ // BODY
F = 4 * C
FC = F // 128
G1, G2 = F // GROUPS, C // GROUPS
HT = QN // 2
BTILES = 6
VN = 2 * C + 2
EPS_C, EPS_T, EPS_Q, QB = 1e-6, 1e-5, 1e-5, 128.0
QCLIP = float(np.float32(QB - EPS_Q))
NORM_FLOOR = 1e-24
START = 16
LOADS = 14
POOL_SETS = 6
DVE_SUMS, DVE_SIGNS, DVE_ALL = 4, 20, 24
CONSTS = {}


def shape_constants():
    parts = {"ident": np.eye(128), "ones": np.ones((128, 128))}
    j, m = np.meshgrid(np.arange(HM), np.arange(HM), indexing="ij")
    same = j // CENTERS == m // CENTERS
    parts["first"] = np.where(same & (j < m), 1.0, 0.0) - np.eye(HM)
    back = np.zeros((128, T, BN))
    back[:, :, 0:TN] = np.eye(128)[:, None, 0:TN]
    for t in range(T):
        for p in range(TN):
            row, col = ROWS_T * t + p // QS, p % QS
            back[p, t, TN + row // PW * 4 + col // PW] = 1.0 / (PW * PW)
    parts["back"] = back.reshape(128, -1)
    p = np.arange(128)
    parts["head_of_row"] = np.stack([p < HD, (p >= HD) & (p < 2 * HD)], 1)
    parts["head_of_center"] = np.stack([p // CENTERS % 2 == 0, p // CENTERS % 2 == 1], 1)
    parts["bias_part"] = np.stack([p == C, p == C + 1], 1)
    parts["last_row"] = np.stack([p == C, p == C], 1)
    at = 0
    for name, a in parts.items():
        CONSTS[name] = (at, a.shape[1])
        at += a.shape[1]
    return np.concatenate([a.astype(np.float32) for a in parts.values()], 1)


SHAPE_CONSTANTS = shape_constants()


def build(nc, x, Wf, bf, Wv, bv, Wp, bp, alpha, beta, W1, b1, W2, b2, consts, out):
    f32, f16, bf16 = mybir.dt.float32, mybir.dt.float16, mybir.dt.bfloat16
    ALU, ACT, AX = mybir.AluOpType, mybir.ActivationFunctionType, mybir.AxisListType
    MAX = bass.bass_isa.ReduceOp.max
    ctx = ExitStack()
    with ctx:
        def sb(name, shape, dt=f32):
            return ctx.enter_context(nc.sbuf_tensor(name, shape, dt))

        def sem(name):
            return ctx.enter_context(nc.semaphore(name))

        ps = ctx.enter_context(nc.psum_tensor("ps", [128, 8, 512], f32))

        xbuf = sb("xbuf", [C, XB, HALF])
        tok = sb("tok", [C + 2, GQ, 2, QN], f16)
        tq = sb("tq", [C, 2, QN])
        xnT = sb("xnT", [TN, 4, T, C + 1])
        xn = sb("xn", [C + 1, 2, QN])
        cenx = sb("cenx", [C + 1, 4, CENTERS])
        cbd = sb("cbd", [C, 2, 4, 2, CENTERS])
        csq = sb("csq", [C, 2, HM])
        cn2 = sb("cn2", [HM, 2])
        cinv = sb("cinv", [HM, 2])
        qT = sb("qT", [HM, C + 1])
        Q = sb("Q", [C + 1, 2, HM])
        sq = sb("sq", [TN, T, D])
        n2 = sb("n2", [TN, T * HEADS])
        n2c, ny2, nxy = (sb(n, [TN, T * HEADS]) for n in ("n2c", "ny2", "nxy"))
        ninv = sb("ninv", [TN, T * HEADS])
        cosb = sb("cosb", [TN, T * HM])
        sig = sb("sig", [TN, 2, T * HM])
        top = sb("top", [TN, T * HEADS])
        eq = sb("eq", [TN, T * HM], bf16)
        eqT = sb("eqT", [HM, QN], bf16)
        sim = sb("sim", [TN, 2, T * HM])
        uT = sb("uT", [C + 1, HM])
        rden = sb("rden", [HM, 1])
        hmul = sb("hmul", [HM, 2])
        a1 = sb("a1", [HM, C])
        aggp = sb("aggp", [HM, C])
        nT = sb("nT", [TN, 2, T, C + 2])
        st = {s: sb(f"st_{s}", [TN, 2, T, 6]) for s in "xt"}
        mo = {s: sb(f"mo_{s}", [TN, 2, 10, T]) for s in "xt"}
        hmax = sb("hmax", [128, GQ * 2 * FC])
        ymax = sb("ymax", [C, GQ * 2])
        gam = sb("gam", [128, 2, 2])
        den = sb("den", [128, 2, 2])
        scale = sb("scale", [128, 2])
        turns = sb("turns", [128, 11 * FC * HT // 2])
        cst = sb("cst", [128, SHAPE_CONSTANTS.shape[1]])
        ident16 = sb("ident16", [128, 128], bf16)
        first16 = sb("first16", [HM, HM], bf16)
        halfpow = sb("halfpow", [128, HM])
        wf = sb("wf", [C, 4, C + 1])
        wfT = sb("wfT", [C + 1, D])
        V = sb("V", [C + 1, 4, VN])
        b1h = sb("b1h", [C + 2, F], f16)
        wsum1, wsum2 = sb("wsum1", [G1, GROUPS]), sb("wsum2", [G2, GROUPS])
        wmean1, wmean2 = sb("wmean1", [G1, GROUPS]), sb("wmean2", [G2, GROUPS])
        w1T = sb("w1T", [C + 2, F], f16)
        w2T = sb("w2T", [128, FC, C], f16)
        b2c, bpc = sb("b2c", [C, 1]), sb("bpc", [C, 1])
        alphac, betac = sb("alphac", [HM, 1]), sb("betac", [TN, 1])

        def const(name, rows=128):
            at, n = CONSTS[name]
            return cst[0:rows, at:at + n]

        def bank(b, rows, n, at=0):
            return ps[0:rows, b, at:at + n]

        def pair(b, rows, n):
            return ps[0:rows, b:b + 2, :].rearrange("p b n -> p (b n)")[:, 0:n]

        ident, ones = const("ident"), const("ones")
        backm = const("back", TN).rearrange("p (t n) -> p t n", t=T)
        y32 = tok[:, :, :, :].rearrange("p q s n -> p (q s n)").bitcast(f32).rearrange("p (q n) -> p q n", n=QN)

        gel = turns[:, 0:3 * FC * HT].rearrange("p (s n) -> p s n", s=3)
        parts = turns[:, 3 * FC * HT:].bitcast(f16).rearrange("p (s n) -> p s n", s=5)
        ghi, glo = parts[:, 0:3, :], parts[:, 3:5, :]
        xq = turns[0:C, 3 * FC * HT:3 * FC * HT + 2 * QN].rearrange("p (s n) -> p s n", s=2)
        simT = turns[0:HM, 3 * FC * HT + 2 * QN:3 * FC * HT + 3 * QN]
        fin = turns[0:C, 0:2 * HALF].rearrange("p (s n) -> p s n", s=2)

        room = [0]

        def early(rows, *shape):
            n = int(np.prod(shape))
            a = y32.rearrange("p q n -> p (q n)")[0:rows, room[0]:room[0] + n]
            room[0] += n
            names = "abc"[:len(shape)]
            return a.rearrange(f"p ({' '.join(names)}) -> p {' '.join(names)}", **dict(zip(names, shape)))

        wv, wp = early(C, 4, C + 1), early(C, D)
        wph = early(C, 4, 2, C)
        w1, gt1, w2, gt2 = early(G1, GROUPS, C), early(G1, GROUPS, C), early(G2, GROUPS, F), early(G2, GROUPS, F)
        b1s, b1l = early(C + 2, F), early(C + 2, F)

        NAMES = """x_side x_T x_stats x_sum x_dif x_m2 x_half x_d2 x_v x_var x_rstd x_shift x_norm0 x_norm xn_ps0 xn_ps
            xn_copied0 xn_copied cen_x cen_f cen_bd cen_sq q_ps cen_n2 cen_inv q_scaled q_T q_done s_ps n2_done
            n2_floor n_newton0 n_square0 n_part0 n_factor0 n_newton1 n_square1 n_part1 n_factor1 n_newton2 n_square2
            n_part2 n_factor2 n_newton3 cos_done sig_done top_done eq_done eqT_ps eqT_copied first_ps sim_done
            simT_ps0 simT_ps simT_copied0 simT_copied u_ps u_done a_ps a_rden a_mul a_half a_done o_ps0 o_ps t_done
            t_placed t_T t_stats t_sum t_dif t_m2 t_half t_d2 t_v t_var t_rstd t_shift t_norm0 t_norm n_ps0 n_ps
            n_hi0 n_hi n_lo0 n_lo c_min final""".split()
        S = {n: sem("s_" + n) for n in NAMES}
        f_ps, f_sq = sem("f_ps"), sem("f_sq")
        h_ps, h_max = sem("h_ps"), sem("h_max")
        bh_ps, b_gelu, b_high, b_hi, b_mid, b_lo, by_ps, b_y, b_ymax = (
            sem(n) for n in ("bh_ps", "b_gelu", "b_high", "b_hi", "b_mid", "b_lo", "by_ps", "b_y", "b_ymax"))
        STARTED = [*S.values(), f_ps, f_sq, h_ps, h_max, bh_ps, b_gelu, b_high, b_hi, b_mid, b_lo, by_ps, b_y, b_ymax]
        x_in = [sem(f"x_in{j}") for j in range(XB)]
        t_out = [sem(f"t_out{j}") for j in range(XB)]
        waited = sem("waited")
        f_in = [sem(f"f_in{i}") for i in range(2)]
        f_out = [sem(f"f_out{i}") for i in range(2)]
        g_max, g_all, g_eps, g_rec, g_scale = (sem(n) for n in ("g_max", "g_all", "g_eps", "g_rec", "g_scale"))
        w_loaded, pe_set, dve_set, pool_set = sem("w_loaded"), sem("pe_set"), sem("dve_set"), sem("pool_set")

        BANKS = ((0, TA, 0, NA, "0"), (TA, T, NA, QN, ""))

        def done(eng, name, q):
            eng.wait_ge(S[name], q + (START + 1))

        X, M, A, R = 3, 2, 1, 0
        FFN, FINAL = "ffn", "final"

        def pipeline(eng, g, part, steps):
            left_out = {"first": FINAL, "middle": None, "last": FFN}[part]
            steps = [s[:3] for s in steps if left_out is None or left_out not in s]

            def slots(js, body, runs):
                for j in js:
                    for phase, lag, step in steps:
                        d = j - lag + phase
                        if runs(j - lag, d):
                            step(d % BODY, g * GQ + body * BODY + d, body * BODY + d, g * BODIES + body + d // BODY)
            if part == "last":
                slots(range(BODY + 1), 0, lambda n, d: n >= 0 and d < BODY)
                return
            slots(range(-X if part == "first" else 0, BODY), 0, lambda n, d: d >= 0 and (n >= 0 or part == "first"))
            with eng.Fori(1, BODIES) as b:
                slots(range(BODY), b, lambda n, d: True)
            slots([BODY], BODIES - 1, lambda n, d: n < BODY)

        def second_pass(eng, g, steps):
            def slots(js, body, runs):
                for j in js:
                    for lag, step in steps:
                        d = j - lag
                        if runs(d):
                            step(d % BTILES, g * (2 * GQ) + body * BTILES + d, body * (BTILES // 2) + d // 2)
            bodies = 2 * GQ // BTILES
            slots(range(BTILES), 0, lambda d: d >= 0)
            with eng.Fori(1, bodies) as b:
                slots(range(BTILES), b, lambda d: True)
            slots(range(BTILES, BTILES + max(lag for lag, _ in steps)), bodies - 1, lambda d: d < BTILES)

        def y_tile(k, place):
            return y32[0:C, bass.ds(place, 1), k % 2 * HT:(k % 2 + 1) * HT].rearrange("c a n -> c (a n)")

        def image_rows(k, lo=0, n=QS):
            v = xbuf[:, k // 2, :].rearrange("c (r w) -> c r w", w=SIDE)
            return v[:, lo:lo + n, k % 2 * QS:(k % 2 + 1) * QS]

        def heads(ap):
            return ap.rearrange("p (h m) -> p h m", m=CENTERS)

        def over_centers(ap):
            return ap.unsqueeze(2).broadcast_to([TN, T * HEADS, CENTERS])

        block = ctx.enter_context(nc.Block())

        @block.sync
        def _(sp):
            for s in STARTED:
                sp.sem_inc(s, START)
            per_row = [(cst[:, :], consts), (w1[:, :, :], W1[0:G1 * GROUPS, :].rearrange("(g r) c -> r g c", g=GROUPS)),
                       (w2[:, :, :], W2[0:G2 * GROUPS, :].rearrange("(g r) f -> r g f", g=GROUPS)),
                       (wf[:, :, 0:C], Wf.rearrange("(k r) c -> r k c", k=4)),
                       (wv[:, :, 0:C], Wv.rearrange("(k r) c -> r k c", k=4)),
                       (wf[:, :, C:C + 1], bf.rearrange("(k r a) -> r k a", k=4, a=1)),
                       (wv[:, :, C:C + 1], bv.rearrange("(k r a) -> r k a", k=4, a=1)),
                       (wp[:, :], Wp),
                       (b1s[C:C + 1, :], b1.rearrange("(a f) -> a f", a=1)),
                       (b1s[C + 1:C + 2, :], b1.rearrange("(a f) -> a f", a=1)),
                       (b2c[:, :], b2.rearrange("(c a) -> c a", a=1)), (bpc[:, :], bp.rearrange("(c a) -> c a", a=1)),
                       (alphac[:, :], alpha.rearrange("(c a) -> c a", a=1).broadcast_to([HM, 1])),
                       (betac[:, :], beta.rearrange("(c a) -> c a", a=1).broadcast_to([TN, 1]))]
            assert len(per_row) == LOADS
            with nc.allow_non_contiguous_dma(reason="a bias as a column: a few hundred numbers"):
                for dst, src in per_row:
                    sp.dma_start(dst, src).then_inc(w_loaded, 16)

            x_half = x.rearrange("i c (s h) w -> i s c (h w)", s=2)
            o_half = out.rearrange("i c (s h) w -> i s c (h w)", s=2)

            def half(a, image, j):
                return a[bass.ds(image + j // 2, 1), j % 2, :, :].rearrange("a c n -> c (a n)")

            def load(src, image, j):
                sp.dma_start(xbuf[:, j, :], half(src, image, j)).then_inc(x_in[j], 16)

            def store(image, j):
                sp.dma_start(half(o_half, image, j), xbuf[:, j, :]).then_inc(t_out[j], 16)

            def load_t(image, j):
                sp.dma_start(fin[:, j % 2, :], half(o_half, image, j)).then_inc(f_in[j % 2], 16)

            def store_final(g, b, j):
                done(sp, "final", g * GQ - GQ + b * BODY + (2 * j + 1))
                sp.dma_start(half(o_half, g * GSIZE - GSIZE + b * (XB // 2), j), fin[:, j % 2, :]).then_inc(f_out[j % 2], 16)

            def final_stored(g, b, j):
                sp.wait_ge(f_out[j % 2], ((g * BODIES + b) * 2 + (j // 2 + 1 - 2 * BODIES)) * 16)
                sp.sem_inc(waited, 1)

            def body(g, b, part, ends):
                for j in range(XB):
                    image = g * GSIZE + b * (XB // 2)
                    if part != "first":
                        store_final(g, b, j)
                    done(sp, "t_placed", g * GQ + b * BODY + (2 * j + 1))
                    store(image, j)
                    sp.wait_ge(t_out[j], (g * BODIES + b) * 16 + 16)
                    sp.sem_inc(waited, 1)
                    load(x_half, image + XB // 2, j)
                    if part != "first":
                        final_stored(g, b, j)
                        if not (ends and j >= 2):
                            load_t(image - GSIZE, j + 2)

            def begin(g):
                sp.wait_ge(by_ps, g * (2 * GQ) + START)
                sp.sem_inc(waited, 1)
                for j in range(2):
                    load_t(g * GSIZE - GSIZE, j)

            def group(g, part):
                with sp.Fori(0, BODIES - 1) as b:
                    body(g, b, part, False)
                body(g, BODIES - 1, part, True)

            for j in range(XB):
                load(x_half, 0, j)
            group(0, "first")
            with sp.Fori(1, GROUPS) as g:
                begin(g)
                group(g, "middle")
            begin(GROUPS)
            for h in range(XB * BODIES):
                b, j = h // XB, h % XB
                store_final(GROUPS, b, j)
                final_stored(GROUPS, b, j)
                if h + 2 < XB * BODIES:
                    load_t(GROUPS * GSIZE - GSIZE + b * (XB // 2), j + 2)
                if h % 3 == 2:
                    done(sp, "t_placed", GROUPS * GQ + (2 * (h // 3) + 1))
                    store(GROUPS * GSIZE, h // 3)
            for j in range(XB):
                sp.wait_ge(t_out[j], (GROUPS * BODIES + 1) * 16)

        @block.gpsimd
        def _(pool):
            nc.gpsimd.memset(halfpow[:, :], -0.5).then_inc(pool_set, 1)
            nc.gpsimd.memset(xnT[:, :, :, C:C + 1], 1.0).then_inc(pool_set, 1)
            nc.gpsimd.memset(nT[:, :, :, C:C + 2], 1.0).then_inc(pool_set, 1)
            nc.gpsimd.memset(w1T[:, :], 0.0).then_inc(pool_set, 1)
            nc.gpsimd.memset(w2T[:, :, :], 0.0).then_inc(pool_set, 1)
            nc.gpsimd.memset(gam[:, :, :], 0.0).then_inc(pool_set, 1)
            pool.wait_ge(pool_set, POOL_SETS)

            def met():
                pool.sem_inc(waited, 1)

            def moments(s, eps):
                def step(k, q, place, use):
                    b = k % 2
                    a, w = st[s][:, b, :, :], mo[s][:, b, :, :]
                    done(pool, s + "_stats", q)
                    done(pool, s + "_norm", q - 2)
                    nc.gpsimd.tensor_tensor(w[:, 0, :], a[:, :, 1], a[:, :, 4], ALU.add).then_inc(S[s + "_sum"], 1)
                    nc.gpsimd.tensor_tensor(w[:, 1, :], a[:, :, 1], a[:, :, 4], ALU.subtract).then_inc(S[s + "_dif"], 1)
                    nc.gpsimd.tensor_tensor(w[:, 2, :], a[:, :, 2], a[:, :, 5], ALU.add).then_inc(S[s + "_m2"], 1)
                    done(pool, s + "_sum", q)
                    done(pool, s + "_dif", q)
                    met()
                    nc.gpsimd.tensor_scalar(w[:, 3:5, :], w[:, 0:2, :], -0.5, 0.0, ALU.mult, ALU.add)\
                        .then_inc(S[s + "_half"], 1)
                    done(pool, s + "_m2", q)
                    met()
                    nc.gpsimd.tensor_scalar(w[:, 6, :], w[:, 2, :], 1.0 / C, eps, ALU.mult, ALU.add).then_inc(S[s + "_v"], 1)
                    done(pool, s + "_half", q)
                    nc.gpsimd.tensor_tensor(w[:, 5, :], w[:, 4, :], w[:, 4, :], ALU.mult).then_inc(S[s + "_d2"], 1)
                    done(pool, s + "_d2", q)
                    done(pool, s + "_v", q)
                    nc.gpsimd.tensor_tensor(w[:, 7, :], w[:, 5, :], w[:, 6, :], ALU.add).then_inc(S[s + "_var"], 1)
                    done(pool, s + "_var", q)
                    nc.gpsimd.tensor_tensor(w[:, 8, :], w[:, 7, :], halfpow[0:TN, 0:T], ALU.pow).then_inc(S[s + "_rstd"], 1)
                    done(pool, s + "_rstd", q)
                    nc.gpsimd.tensor_tensor(w[:, 9, :], w[:, 3, :], w[:, 8, :], ALU.mult).then_inc(S[s + "_shift"], 1)
                return step

            def center_squares(k, q, place, use):
                b = k % 2
                done(pool, "cen_bd", q)
                done(pool, "q_ps", q - 2)
                v = cbd[:, b, :, :, :].rearrange("c k h m -> c (k h m)")
                nc.gpsimd.tensor_tensor(csq[:, b, :], v, v, ALU.mult).then_inc(S["cen_sq"], 1)

            def norm_guess(k, q, place, use):
                done(pool, "n2_done", q)
                met()
                nc.gpsimd.tensor_scalar(n2c[:, :], n2[:, :], NORM_FLOOR, 0.0, ALU.max, ALU.add).then_inc(S["n2_floor"], 1)
                done(pool, "n2_floor", q)
                done(pool, "cos_done", q - 1)
                met()
                i32 = mybir.dt.int32
                nc.gpsimd.tensor_scalar(ninv[:, :].bitcast(i32), n2c[:, :].bitcast(i32), -0.5, float(0x5F3759DF),
                                        ALU.mult, ALU.add).then_inc(S["n_newton0"], 1)

            def newton(i):
                def step(k, q, place, use):
                    done(pool, f"n_newton{i}", q)
                    nc.gpsimd.tensor_tensor(ny2[:, :], ninv[:, :], ninv[:, :], ALU.mult).then_inc(S[f"n_square{i}"], 1)
                    done(pool, f"n_square{i}", q)
                    nc.gpsimd.tensor_tensor(nxy[:, :], ny2[:, :], n2c[:, :], ALU.mult).then_inc(S[f"n_part{i}"], 1)
                    done(pool, f"n_part{i}", q)
                    met()
                    nc.gpsimd.tensor_scalar(nxy[:, :], nxy[:, :], -0.5, 1.5, ALU.mult, ALU.add)\
                        .then_inc(S[f"n_factor{i}"], 1)
                    done(pool, f"n_factor{i}", q)
                    nc.gpsimd.tensor_tensor(ninv[:, :], ninv[:, :], nxy[:, :], ALU.mult).then_inc(S[f"n_newton{i + 1}"], 1)
                return step

            def center_norms(k, q, place, use):
                b = k % 2
                done(pool, "cen_n2", q)
                done(pool, "q_done", q - 2)
                nc.gpsimd.tensor_tensor(cinv[:, b:b + 1], cn2[:, b:b + 1], halfpow[0:HM, 0:1], ALU.pow).then_inc(S["cen_inv"], 1)

            def over_partitions(n, i):
                pool.wait_ge(g_max, n)
                met()
                nc.gpsimd.partition_all_reduce(gam[:, i, 1:2], gam[:, i, 0:1], 128, MAX).then_inc(g_all, 1)

            def marks(k, q, place, use):
                done(pool, "top_done", q)
                done(pool, "eqT_ps", q - 1)
                nc.gpsimd.tensor_tensor(heads(eq[:, :]), heads(sig[:, k % 2, :]), over_centers(top[:, :]), ALU.subtract)\
                    .then_inc(S["eq_done"], 1)

            attention = [(X, 1, moments("x", EPS_C)), (M, 1, norm_guess), (M, 1, newton(0)), (M, 1, newton(1)),
                         (M, 1, newton(2)), (X, 1, center_squares), (X, 1, center_norms), (A, 0, marks),
                         (R, 0, moments("t", EPS_T), FFN)]

            def group(g, part):
                pipeline(pool, g, part, attention)
                over_partitions(2 * g + 1, 0)

                def middle_chunk(k, i, place):
                    pool.wait_ge(b_gelu, i + (START + 1))
                    pool.wait_ge(by_ps, i + (START - 2))
                    met()
                    nc.gpsimd.tensor_copy(ghi[:, k % 3, HT:2 * HT], gel[:, k % 3, HT:2 * HT]).then_inc(b_mid, 1)

                second_pass(pool, g, [(0, middle_chunk)])
                over_partitions(2 * g + 2, 1)

            group(0, "first")
            with pool.Fori(1, GROUPS) as g:
                group(g, "middle")
            pipeline(pool, GROUPS, "last", attention)

        @block.scalar
        def _(act):
            def normalise(s, b0, part):
                t0, t1, _, _, end = BANKS[part]

                def step(k, q, place, use):
                    if part == 0:
                        done(act, s + "_shift", q)
                        if s == "x":
                            done(act, "u_ps", q - 4)
                        else:
                            done(act, "n_ps", q - 2)
                    m = mo[s][:, k % 2, :, :]
                    for t in range(t0, t1):
                        dst = xnT[:, k % 4, t, 0:C] if s == "x" else nT[:, k % 2, t, 0:C]
                        ins = nc.scalar.activation(dst, bank(b0 + part, TN, C, (t - t0) * C), ACT.Identity,
                                                   bias=m[:, 9, t:t + 1], scale=m[:, 8, t:t + 1])
                    ins.then_inc(S[s + "_norm" + end], 1)
                return step

            def gather(k, q, place, use):
                if k % 2 == 0:
                    act.wait_ge(x_in[k // 2], use * 16 + 16)
                done(act, "x_T", q - 2)
                nc.scalar.copy(xq[:, k % 2, :].rearrange("c (r w) -> c r w", w=QS), image_rows(k))\
                    .then_inc(S["x_side"], 1)

            def place_t(k, q, place, use):
                done(act, "t_done", q)
                nc.scalar.copy(image_rows(k), tq[:, k % 2, :].rearrange("c (r w) -> c r w", w=QS))\
                    .then_inc(S["t_placed"], 1)

            def copy_x(part):
                _, _, lo, hi, end = BANKS[part]

                def step(k, q, place, use):
                    done(act, "xn_ps" + end, q)
                    if part == 0:
                        done(act, "s_ps", q - 2)
                    n = (hi - lo) // TN
                    src = bank(part, C + 1, n * BN).rearrange("c (t n) -> c t n", n=BN)[:, :, 0:TN]
                    nc.scalar.copy(xn[:, k % 2, lo:hi].rearrange("c (t n) -> c t n", t=n), src)\
                        .then_inc(S["xn_copied" + end], 1)
                return step

            def squares(t0, t1):
                def step(k, q, place, use):
                    if t0 == 0:
                        done(act, "n2_done", q - 1)
                    for t in range(t0, t1):
                        act.wait_ge(f_ps, q * T + (START + t + 1))
                        nc.scalar.activation(sq[:, t, :], bank(2 + t % 2, TN, D), ACT.Square).then_inc(f_sq, 1)
                return step

            def sigmoid(k, q, place, use):
                done(act, "cos_done", q)
                done(act, "sim_done", q - 2)
                nc.scalar.activation(sig[:, k % 2, :], cosb[:, :], ACT.Sigmoid, bias=betac[:, :]).then_inc(S["sig_done"], 1)

            def copy_eq(k, q, place, use):
                done(act, "eqT_ps", q)
                done(act, "first_ps", q - 1)
                nc.scalar.activation(eqT[:, :], ps[:, 4, :].bitcast(bf16)[:, 0:QN], ACT.Relu, bias=ones[0:HM, 0:1],
                                     scale=2.0 ** 127).then_inc(S["eqT_copied"], 1)

            def copy_sim(part):
                _, _, lo, hi, end = BANKS[part]

                def step(k, q, place, use):
                    done(act, "simT_ps" + end, q)
                    if part == 0:
                        done(act, "o_ps", q - 1)
                    nc.scalar.copy(simT[:, lo:hi], bank(4 + part, HM, hi - lo)).then_inc(S["simT_copied" + end], 1)
                return step

            def n_high(half, part):
                _, _, lo, hi, end = BANKS[half]

                def step(k, q, place, use):
                    done(act, "n_ps" + end, q)
                    if part != "first" and half == 0:
                        done(act, "final", q - GQ)
                    o = tok[:, bass.ds(place, 1), 0, lo:hi].rearrange("p a n -> p (a n)")
                    nc.scalar.copy(o, bank(6 + half, C + 2, hi - lo)).then_inc(S["n_hi" + end], 1)
                return step

            def attention(part):
                return [(R, 1, normalise("t", 6, 1), FFN), (A, 1, copy_sim(0)), (R, 1, n_high(0, part), FFN),
                        (A, 1, copy_sim(1)), (R, 1, n_high(1, part), FFN), (X, 1, normalise("x", 0, 0)),
                        (X, 1, normalise("x", 0, 1)), (R, 1, place_t), (X, 1, copy_x(0)), (X, 1, copy_x(1)),
                        (A, 0, sigmoid), (M, 0, squares(0, 2)), (X, 0, gather), (M, 0, squares(2, 5)),
                        (A, 0, copy_eq), (M, 0, squares(5, 7)), (R, 0, normalise("t", 6, 0), FFN)]

            act.wait_ge(w_loaded, 16 * LOADS)

            def group(g, part):
                pipeline(act, g, part, attention(part))
                if part != "first":
                    for i in range(2):
                        act.wait_ge(f_out[i], g * (16 * GSIZE))

                def gelu(k, i, place):
                    act.wait_ge(bh_ps, i + (START + 1))
                    act.wait_ge(b_lo, i + (START - 2))
                    h = 3 * (k % 2)
                    nc.scalar.activation(gel[:, k % 3, :].rearrange("p (c n) -> p c n", c=FC), ps[:, h:h + 3, 0:HT],
                                         ACT.Gelu, scale=scale[:, 0:1]).then_inc(b_gelu, 1)
                    act.wait_ge(by_ps, i + (START - 2))
                    nc.scalar.activation(ghi[:, k % 3, 2 * HT:], ps[:, h + 2, 0:HT], ACT.Gelu, scale=scale[:, 0:1])\
                        .then_inc(b_high, 1)

                def y_out(k, i, place):
                    act.wait_ge(by_ps, i + (START + 1))
                    nc.scalar.activation(y_tile(k, place), bank(6 + k % 2, C, HT), ACT.Identity, bias=b2c[:, :])\
                        .then_inc(b_y, 1)

                act.wait_ge(g_scale, 2 * g + 1)
                second_pass(act, g, [(0, gelu), (3, y_out)])

            group(0, "first")
            with act.Fori(1, GROUPS) as g:
                group(g, "middle")
            pipeline(act, GROUPS, "last", attention("last"))

        @block.vector
        def _(dve):
            count = [0]

            def step(ins):
                count[0] += 1
                ins.then_inc(dve_set, 1)
                dve.wait_ge(dve_set, count[0])

            v = nc.vector
            dve.wait_ge(w_loaded, 16 * LOADS)
            dve.wait_ge(pool_set, POOL_SETS)
            step(v.tensor_copy(ident16[:, :], ident))
            step(v.tensor_copy(first16[:, :], const("first")))
            for w, gt, total, mean, n in ((w1, gt1, wsum1, wmean1, G1 * C), (w2, gt2, wsum2, wmean2, G2 * F)):
                step(v.reduce_sum(total[:, :], w[:, :, :], AX.X))
            assert count[0] == DVE_SUMS
            dve.wait_ge(pe_set, 1)
            step(v.tensor_scalar(wmean1[:, :], bank(0, G1, GROUPS), 1.0 / (G1 * C), None, ALU.mult))
            step(v.tensor_scalar(wmean2[:, :], bank(1, G2, GROUPS), 1.0 / (G2 * F), None, ALU.mult))
            for w, gt, mean, rows, n in ((w1, gt1, wmean1, G1, C), (w2, gt2, wmean2, G2, F)):
                m = mean[:, :].unsqueeze(2).broadcast_to([rows, GROUPS, n])
                step(v.tensor_tensor(gt[:, :, :], w[:, :, :], m, ALU.is_gt))
                step(v.tensor_tensor(w[:, :, :], w[:, :, :], m, ALU.is_lt))
                step(v.tensor_tensor(w[:, :, :], gt[:, :, :], w[:, :, :], ALU.subtract))
            step(v.tensor_copy(wfT[:, :], bank(2, C + 1, D)))
            wpT = bank(3, C, D).rearrange("r (k o) -> r k o", k=4)
            for h in range(2):
                step(v.tensor_scalar(wph[:, :, h, :], wpT, const("head_of_row", C)[:, h:h + 1], None, ALU.mult))
            step(v.tensor_copy(V[:, :, 2 * C:VN], const("last_row", C + 1).unsqueeze(1).broadcast_to([C + 1, 4, 2])))
            r, m = slice(C, C + 2), const("bias_part")
            step(v.tensor_copy(b1h[r, :], b1s[r, :]))
            step(v.tensor_tensor(b1l[r, :], b1s[r, :], b1h[r, :], ALU.subtract))
            step(v.tensor_scalar(b1l[r, :], b1l[r, :], m[r, 1:2], None, ALU.mult))
            step(v.scalar_tensor_tensor(w1T[r, :], b1h[r, :], m[r, 0:1], b1l[r, :], ALU.mult, ALU.add))
            assert count[0] == DVE_SIGNS
            dve.wait_ge(pe_set, 2)
            for i in range(2):
                step(v.tensor_copy(V[:, 2 * i:2 * i + 2, 0:2 * C],
                                   bank(4 + i, C + 1, 4 * C).rearrange("c (k o) -> c k o", k=2)))
            step(v.tensor_copy(w1T[0:C, 0:G1 * GROUPS], bank(6, C, G1 * GROUPS)))
            step(v.tensor_copy(w2T[:, :, 0:G2 * GROUPS],
                               bank(7, 128, FC * C).rearrange("f (c o) -> f c o", c=FC)[:, :, 0:G2 * GROUPS]))
            assert count[0] == DVE_ALL

            def stats(s, b0):
                def step(k, q, place, use):
                    done(dve, s + "_T", q)
                    done(dve, s + "_rstd", q - 2)
                    for t in range(T):
                        src = bank(b0, TN, C, t * C) if t < TA else bank(b0 + 1, TN, C, (t - TA) * C)
                        last_one = v.bn_stats(st[s][:, k % 2, t, :], src)
                    last_one.then_inc(S[s + "_stats"], 1)
                return step

            def pooled(k, q, place, use):
                done(dve, "xn_copied", q)
                done(dve, "u_done", q - 4)
                sums = pair(0, C + 1, T * BN).rearrange("c (t n) -> c n t", n=BN)[:, TN:BN, :]
                v.reduce_sum(cenx[:, k % 4, :], sums, AX.X).then_inc(S["cen_x"], 1)

            def centers(k, q, place, use):
                done(dve, "cen_f", q)
                done(dve, "q_ps", q - 2)
                f = bank(0, C, 4 * CENTERS).rearrange("r (k m) -> r k m", k=4)
                mask = const("head_of_row", C)
                v.tensor_tensor(cbd[:, k % 2, :, :, :], f.unsqueeze(2).broadcast_to([C, 4, 2, CENTERS]),
                                mask.unsqueeze(1).unsqueeze(3).broadcast_to([C, 4, 2, CENTERS]), ALU.mult)\
                    .then_inc(S["cen_bd"], 1)

            def center_floor(k, q, place, use):
                done(dve, "q_ps", q)
                done(dve, "cen_inv", q - 2)
                v.tensor_scalar(cn2[:, k % 2:k % 2 + 1], bank(0, HM, 1, 64), NORM_FLOOR, None, ALU.max)\
                    .then_inc(S["cen_n2"], 1)

            def q_scaled(k, q, place, use):
                done(dve, "cen_inv", q)
                v.tensor_scalar(qT[:, :], bank(0, HM, C + 1, 128), cinv[:, k % 2:k % 2 + 1], alphac[:, :],
                                ALU.mult, ALU.mult).then_inc(S["q_scaled"], 1)

            def q_placed(k, q, place, use):
                done(dve, "q_T", q)
                done(dve, "s_ps", q - 2)
                v.tensor_copy(Q[:, k % 2, :], bank(0, C + 1, HM, 256)).then_inc(S["q_done"], 1)

            def norms(t0, t1):
                def step(k, q, place, use):
                    dve.wait_ge(f_sq, q * T + (START + t1))
                    if t0 == 0:
                        done(dve, "n2_floor", q - 1)
                    ins = v.reduce_sum(n2[:, t0 * HEADS:t1 * HEADS],
                                       sq[:, t0:t1, :].rearrange("p t (h d) -> p (t h) d", d=HD), AX.X)
                    if t1 == T:
                        ins.then_inc(S["n2_done"], 1)
                return step

            def cosine(k, q, place, use):
                done(dve, "s_ps", q)
                done(dve, "n_newton3", q)
                done(dve, "sig_done", q - 1)
                v.tensor_tensor(heads(cosb[:, :]), heads(pair(2, TN, T * HM)), over_centers(ninv[:, :]), ALU.mult)\
                    .then_inc(S["cos_done"], 1)

            def maxima(k, q, place, use):
                done(dve, "sig_done", q)
                v.tensor_reduce(top[:, :], heads(sig[:, k % 2, :]), AX.X, ALU.max).then_inc(S["top_done"], 1)

            def masked(k, q, place, use):
                done(dve, "first_ps", q)
                done(dve, "u_ps", q - 2)
                v.scalar_tensor_tensor(sim[:, k % 2, :], pair(4, TN, T * HM), -1.0, sig[:, k % 2, :],
                                       ALU.is_equal, ALU.mult).then_inc(S["sim_done"], 1)

            def summed(k, q, place, use):
                done(dve, "u_ps", q)
                done(dve, "a_ps", q - 1)
                v.tensor_tensor(heads(uT[:, :]), heads(bank(4, C + 1, HM)),
                                cenx[:, k % 4, :].unsqueeze(1).broadcast_to([C + 1, HEADS, CENTERS]), ALU.add)\
                    .then_inc(S["u_done"], 1)

            def denominators(k, q, place, use):
                done(dve, "a_ps", q)
                v.reciprocal(rden[:, :], bank(5, HM, 1, 2 * C)).then_inc(S["a_rden"], 1)

            def factors(k, q, place, use):
                done(dve, "a_rden", q)
                v.tensor_scalar(hmul[:, :], const("head_of_center"), rden[:, :], None, ALU.mult).then_inc(S["a_mul"], 1)

            def first_heads(k, q, place, use):
                done(dve, "a_mul", q)
                v.tensor_scalar(a1[:, :], bank(5, HM, C), hmul[:, 0:1], None, ALU.mult).then_inc(S["a_half"], 1)

            def second_heads(k, q, place, use):
                done(dve, "a_half", q)
                done(dve, "o_ps", q - 1)
                v.scalar_tensor_tensor(aggp[:, :], bank(5, HM, C, C), hmul[:, 1:2], a1[:, :], ALU.mult, ALU.add)\
                    .then_inc(S["a_done"], 1)

            def residual(half, part):
                _, _, lo, hi, end = BANKS[half]

                def step(k, q, place, use):
                    done(dve, "o_ps" + end, q)
                    if half == 0:
                        done(dve, "t_placed", q - 2)
                        if part != "last":
                            done(dve, "t_T", q - 2)
                    o = bank(4 + half, C, hi - lo).rearrange("c (r w) -> c r w", w=QS)
                    t = tq[:, k % 2, lo:hi].rearrange("c (r w) -> c r w", w=QS)
                    ins = v.scalar_tensor_tensor(t, o, bpc[:, :], image_rows(k, lo // QS, (hi - lo) // QS), ALU.add, ALU.add)
                    if half == 1:
                        ins.then_inc(S["t_done"], 1)
                return step

            def n_low(half):
                _, _, lo, hi, end = BANKS[half]

                def step(k, q, place, use):
                    done(dve, "n_hi" + end, q)
                    high, low = (tok[:, bass.ds(place, 1), i, lo:hi].rearrange("p a n -> p (a n)") for i in range(2))
                    v.tensor_tensor(low, bank(6 + half, C + 2, hi - lo), high, ALU.subtract).then_inc(S["n_lo" + end], 1)
                return step

            def h_largest(u0, u1):
                def step(k, q, place, use):
                    for u in range(u0, u1):
                        dve.wait_ge(h_ps, q * (2 * FC) + (START + u + 1))
                        o = hmax[:, bass.ds(place * (2 * FC) + u, 1)]
                        v.tensor_reduce(o, bank(6 + u % 2, 128, HT), AX.X, ALU.max, apply_absolute_value=True)\
                            .then_inc(h_max, 1)
                return step

            def largest(src, i, rows):
                v.tensor_reduce(gam[0:rows, i, 0:1], src, AX.X, ALU.max).then_inc(g_max, 1)

            def group_scale(n, i):
                dve.wait_ge(g_all, n)
                v.tensor_scalar(den[:, i, 0:1], gam[:, i, 1:2], EPS_Q, None, ALU.add).then_inc(g_eps, 1)
                dve.wait_ge(g_eps, n)
                v.reciprocal(den[:, i, 1:2], den[:, i, 0:1]).then_inc(g_rec, 1)
                dve.wait_ge(g_rec, n)
                v.tensor_scalar(scale[:, i:i + 1], den[:, i, 1:2], QB, None, ALU.mult).then_inc(g_scale, 1)

            def y_of(place):
                return y32[0:C, bass.ds(place, 1), :].rearrange("c a n -> c (a n)")

            def scaled(g, part):
                def step(k, q, place, use):
                    if isinstance(place, int) and place == 0:
                        group_scale(2 * g, 1)
                        dve.wait_ge(g_scale, 2 * g)
                    for d in range(3 * place, 3 * place + 3) if part == "last" else (place,):
                        v.tensor_scalar(y_of(d), y_of(d), scale[0:C, 1:2], QCLIP, ALU.mult, ALU.min)\
                            .then_inc(S["c_min"], 1)
                return step

            def finish(part):
                def one(k, q, place, use):
                    if k % 2 == 0:
                        dve.wait_ge(f_in[k // 2 % 2], use * 32 + (k // 4 + 1 - 2 * BODIES) * 16)
                    done(dve, "c_min", q - GQ)
                    t = fin[:, k // 2 % 2, :].rearrange("c (r w) -> c r w", w=SIDE)[:, :, k % 2 * QS:(k % 2 + 1) * QS]
                    v.scalar_tensor_tensor(t, y_of(place).rearrange("c (r w) -> c r w", w=QS), -QCLIP, t,
                                           ALU.max, ALU.add).then_inc(S["final"], 1)

                def step(k, q, place, use):
                    for d in range(3 * place, 3 * place + 3):
                        one(d % BODY, GROUPS * GQ + d, d, GROUPS * BODIES + d // BODY)
                return step if part == "last" else one

            def attention(g, part):
                return [(M, 1, norms(TA, T)), (R, 1, n_low(0), FFN), (R, 1, n_low(1), FFN), (A, 1, summed),
                         (R, 1, h_largest(0, 2), FFN), (A, 1, denominators), (A, 1, factors), (A, 1, first_heads),
                         (R, 1, h_largest(2, 3), FFN), (A, 1, second_heads), (R, 1, h_largest(3, 5), FFN),
                         (X, 1, pooled), (M, 1, cosine), (X, 1, centers), (A, 1, residual(0, part)),
                         (R, 1, h_largest(5, 6), FFN), (A, 1, residual(1, part)), (X, 1, center_floor),
                         (A, 0, maxima), (X, 1, q_scaled), (R, 0, stats("t", 6), FFN),
                         (R, 0, scaled(g, part), FINAL), (X, 1, q_placed), (M, 0, norms(0, TA)),
                         (X, 0, stats("x", 0)), (A, 0, masked), (R, 0, finish(part), FINAL)]

            def group(g, part):
                pipeline(dve, g, part, attention(g, part))
                dve.wait_ge(h_max, g * (GQ * 2 * FC) + (START + GQ * 2 * FC))
                largest(hmax[:, :], 0, 128)
                group_scale(2 * g + 1, 0)
                def first_chunk(k, i, place):
                    dve.wait_ge(b_gelu, i + (START + 1))
                    dve.wait_ge(by_ps, i + (START - 2))
                    v.tensor_copy(ghi[:, k % 3, 0:HT], gel[:, k % 3, 0:HT]).then_inc(b_hi, 1)

                def low_parts(k, i, place):
                    for high in (b_hi, b_mid, b_high):
                        dve.wait_ge(high, i + (START + 1))
                    dve.wait_ge(by_ps, i + (START - 1))
                    v.scalar_tensor_tensor(glo[:, k % 2, :], gel[:, k % 3, :], QCLIP, ghi[:, k % 3, :],
                                           ALU.min, ALU.subtract).then_inc(b_lo, 1)

                def y_largest(k, i, place):
                    dve.wait_ge(b_y, i + (START + 1))
                    v.tensor_reduce(ymax[:, bass.ds(2 * place + k % 2, 1)], y_tile(k, place), AX.X, ALU.max,
                                    apply_absolute_value=True).then_inc(b_ymax, 1)

                second_pass(dve, g, [(0, first_chunk), (4, y_largest), (1, low_parts)])
                dve.wait_ge(b_ymax, g * (2 * GQ) + (START + 2 * GQ))
                largest(ymax[:, :], 1, C)
                dve.sem_inc(waited, 1)

            group(0, "first")
            with dve.Fori(1, GROUPS) as g:
                group(g, "middle")
            pipeline(dve, GROUPS, "last", attention(GROUPS, "last"))

        @block.tensor
        def _(pe):
            mm, tr = nc.tensor.matmul, nc.tensor.transpose
            pe.wait_ge(w_loaded, 16 * LOADS)
            pe.wait_ge(dve_set, DVE_SUMS)
            mm(bank(0, G1, GROUPS), ones[0:G1, 0:G1], wsum1[:, :], start=True, stop=True)
            mm(bank(1, G2, GROUPS), ones[0:G2, 0:G2], wsum2[:, :], start=True, stop=True)
            for k in range(4):
                tr(bank(2, C + 1, C, k * C), wf[:, k, :], ident[0:C, 0:C])
                ins = tr(bank(3, C, C, k * C), wp[:, k * C:(k + 1) * C], ident[0:C, 0:C])
            ins.then_inc(pe_set, 1)
            pe.wait_ge(dve_set, DVE_SIGNS)
            for k in range(4):
                mm(bank(4 + k // 2, C + 1, 2 * C, k % 2 * 2 * C), wv[:, k, :],
                   wph[:, k, :, :].rearrange("r h o -> r (h o)"), start=True, stop=True)
            for g in range(GROUPS):
                tr(bank(6, C, G1, g * G1), w1[:, g, :], ident[0:G1, 0:G1])
                for c in range(FC):
                    ins = tr(bank(7, 128, G2, c * C + g * G2), w2[:, g, c * 128:(c + 1) * 128], ident[0:G2, 0:G2])
            ins.then_inc(pe_set, 1)
            pe.wait_ge(dve_set, DVE_ALL)

            def tile_bank(b0, rows, n, t):
                return bank(b0, rows, n, t * n) if t < TA else bank(b0 + 1, rows, n, (t - TA) * n)

            def to_tokens(s, b0):
                def step(k, q, place, use):
                    if s == "x":
                        done(pe, "x_side", q)
                        done(pe, "q_done", q - 1)
                    else:
                        done(pe, "t_done", q)
                        pe.wait_ge(h_max, q * (2 * FC) + START)
                    for t in range(T):
                        src = (xq if s == "x" else tq)[:, k % 2, t * TN:(t + 1) * TN]
                        ins = tr(tile_bank(b0, TN, C, t), src, ident[0:C, 0:C])
                    ins.then_inc(S[s + "_T"], 1)
                return step

            def x_back(part):
                t0, t1, _, _, end = BANKS[part]

                def step(k, q, place, use):
                    done(pe, "x_norm" + end, q)
                    for t in range(t0, t1):
                        ins = mm(bank(part, C + 1, BN, (t - t0) * BN), xnT[:, k % 4, t, :], backm[:, t, :], start=True, stop=True)
                    ins.then_inc(S["xn_ps" + end], 1)
                return step

            def centers(k, q, place, use):
                done(pe, "cen_x", q)
                done(pe, "xn_copied", q)
                for c in range(4):
                    ins = mm(bank(0, C, CENTERS, c * CENTERS), wfT[:, c * C:(c + 1) * C], cenx[:, k % 4, :],
                             start=True, stop=True)
                ins.then_inc(S["cen_f"], 1)

            def center_products(k, q, place, use):
                done(pe, "cen_bd", q)
                done(pe, "cen_sq", q)
                mm(bank(0, HM, 1, 64), csq[:, k % 2, :], ones[0:C, 0:1], start=True, stop=True)
                n = 2 * CENTERS
                for c in range(4):
                    ins = mm(ps[c * n:(c + 1) * n, 0, 128:128 + C + 1],
                             cbd[:, k % 2, c, :, :].rearrange("r h m -> r (h m)"), wf[:, c, :], start=True, stop=True)
                ins.then_inc(S["q_ps"], 1)

            def q_back(k, q, place, use):
                done(pe, "q_scaled", q)
                tr(bank(0, C + 1, HM, 256), qT[:, :], ident).then_inc(S["q_T"], 1)

            def features(t0, t1):
                def step(k, q, place, use):
                    if t0 == 0:
                        done(pe, "cos_done", q - 1)
                    for t in range(t0, t1):
                        if t in (0, TA):
                            done(pe, "xn_copied0" if t == 0 else "xn_copied", q)
                        if t >= 2:
                            pe.wait_ge(f_sq, q * T + (START + t - 1))
                        mm(bank(2 + t % 2, TN, D), xn[:, k % 2, t * TN:(t + 1) * TN], wfT[:, :], start=True, stop=True)\
                            .then_inc(f_ps, 1)
                return step

            def scores(k, q, place, use):
                pe.wait_ge(f_sq, q * T + (START + T))
                done(pe, "q_done", q)
                for t in range(T):
                    ins = mm(tile_bank(2, TN, HM, t), xn[:, k % 2, t * TN:(t + 1) * TN], Q[:, k % 2, :],
                             start=True, stop=True)
                ins.then_inc(S["s_ps"], 1)

            def marks_back(k, q, place, use):
                done(pe, "eq_done", q)
                done(pe, "t_done", q - 1)
                o = ps[:, 4, :].bitcast(bf16)
                for t in range(T):
                    ins = tr(o[:, t * TN:(t + 1) * TN], eq[:, t * HM:(t + 1) * HM], ident16[0:TN, 0:TN])
                ins.then_inc(S["eqT_ps"], 1)

            def find_first(k, q, place, use):
                done(pe, "eqT_copied", q)
                for t in range(T):
                    ins = mm(tile_bank(4, TN, HM, t), eqT[:, t * TN:(t + 1) * TN], first16[:, :], start=True, stop=True)
                ins.then_inc(S["first_ps"], 1)

            def sim_back(part):
                t0, t1, _, _, end = BANKS[part]

                def step(k, q, place, use):
                    done(pe, "sim_done", q)
                    for t in range(t0, t1):
                        ins = tr(tile_bank(4, HM, TN, t), sim[:, k % 2, t * HM:(t + 1) * HM], ident[0:TN, 0:TN])
                    ins.then_inc(S["simT_ps" + end], 1)
                return step

            def aggregate(k, q, place, use):
                done(pe, "simT_copied0", q)
                for t in range(T):
                    ins = mm(bank(4, C + 1, HM), xnT[:, k % 4, t, :], sim[:, k % 2, t * HM:(t + 1) * HM],
                             start=t == 0, stop=t == T - 1)
                ins.then_inc(S["u_ps"], 1)

            def project(k, q, place, use):
                done(pe, "u_done", q)
                done(pe, "simT_copied", q)
                for c in range(4):
                    n = 2 * CENTERS
                    ins = mm(ps[c * n:(c + 1) * n, 5, 0:VN], uT[:, c * n:(c + 1) * n], V[:, c, :], start=True, stop=True)
                ins.then_inc(S["a_ps"], 1)

            def spread(part):
                _, _, lo, hi, end = BANKS[part]

                def step(k, q, place, use):
                    done(pe, "a_done", q)
                    mm(bank(4 + part, C, hi - lo), aggp[:, :], simT[:, lo:hi], start=True, stop=True)\
                        .then_inc(S["o_ps" + end], 1)
                return step

            def t_back(part):
                t0, t1, _, _, end = BANKS[part]

                def step(k, q, place, use):
                    done(pe, "t_norm" + end, q)
                    for t in range(t0, t1):
                        ins = tr(tile_bank(6, C + 2, TN, t), nT[:, k % 2, t, :], ident[0:TN, 0:TN])
                    ins.then_inc(S["n_ps" + end], 1)
                return step

            def hidden(dst, place, s, c):
                for part in range(2):
                    ins = mm(dst, w1T[:, c * 128:(c + 1) * 128],
                             tok[:, bass.ds(place, 1), part, s * HT:(s + 1) * HT].rearrange("p a n -> p (a n)"),
                             start=part == 0, stop=part == 1)
                return ins

            def hidden_tiles(u0, u1):
                def step(k, q, place, use):
                    for u in range(u0, u1):
                        if u < 2:
                            done(pe, "n_lo0" if u == 0 else "n_lo", q)
                        if u >= 2:
                            pe.wait_ge(h_max, q * (2 * FC) + (START + u - 1))
                        hidden(bank(6 + u % 2, 128, HT), place, u // FC, u % FC).then_inc(h_ps, 1)
                return step

            def attention():
                return [(M, 1, scores), (A, 1, sim_back(0)), (R, 1, t_back(0), FFN), (A, 1, sim_back(1)),
                        (R, 1, t_back(1), FFN), (A, 1, aggregate), (R, 1, hidden_tiles(0, 2), FFN), (A, 1, project),
                        (X, 1, x_back(0)), (R, 1, hidden_tiles(2, 4), FFN), (X, 1, x_back(1)),
                        (R, 1, hidden_tiles(4, 5), FFN), (A, 1, spread(0)), (R, 1, hidden_tiles(5, 6), FFN),
                        (X, 1, centers), (A, 1, spread(1)), (M, 0, features(0, 1)), (X, 1, center_products),
                        (M, 0, features(1, 2)), (R, 0, to_tokens("t", 6), FFN), (M, 0, features(2, 4)),
                        (X, 1, q_back), (M, 0, features(4, 6)), (A, 0, marks_back), (X, 0, to_tokens("x", 0)),
                        (M, 0, features(6, 7)), (A, 0, find_first)]

            def group(g, part):
                pipeline(pe, g, part, attention())
                def up(k, i, place):
                    pe.wait_ge(b_high, i + (START - 1))
                    for c in range(FC):
                        ins = hidden(bank(3 * (k % 2) + c, 128, HT), place, k % 2, c)
                    ins.then_inc(bh_ps, 1)

                def down(k, i, place):
                    pe.wait_ge(b_lo, i + (START + 1))
                    pe.wait_ge(b_y, i + (START - 1))
                    for n, (part, s, c) in enumerate((part, s, c) for part, s in ((ghi, k % 3), (glo, k % 2))
                                                     for c in range(FC)):
                        ins = mm(bank(6 + k % 2, C, HT), w2T[:, c, :], part[:, s, c * HT:(c + 1) * HT],
                                 start=n == 0, stop=n == 2 * FC - 1)
                    ins.then_inc(by_ps, 1)

                done(pe, "q_done", g * GQ + (GQ - 1 + X))
                done(pe, "cos_done", g * GQ + (GQ - 1 + M))
                done(pe, "t_done", g * GQ + (GQ - 1 + A))
                pe.wait_ge(h_max, g * (GQ * 2 * FC) + (START + GQ * 2 * FC))
                second_pass(pe, g, [(0, up), (3, down)])
                pe.wait_ge(b_y, g * (2 * GQ) + (START + 2 * GQ))

            group(0, "first")
            with pe.Fori(1, GROUPS) as g:
                group(g, "middle")
            pipeline(pe, GROUPS, "last", attention())


INPUTS = ["x"] + ["L0_conv_" + n for n in ("Wf", "bf", "Wv", "bv", "Wp", "bp", "sim_alpha", "sim_beta")] \
    + ["L0_ffn_" + n for n in ("W1", "b1", "W2", "b2")]


def kernel(**inputs):
    import concourse.bacc as bacc
    from concourse.bass_utils import run_bass_kernel_spmd

    nc = bacc.Bacc("TRN2", target_bir_lowering=False, num_devices=1)
    arrays = {f"in_{n}": np.ascontiguousarray(inputs[n]) for n in INPUTS}
    arrays["in_constants"] = SHAPE_CONSTANTS
    args = [nc.dram_tensor(n, a.shape, mybir.dt.from_np(a.dtype), kind="ExternalInput").ap() for n, a in arrays.items()]
    args.append(nc.dram_tensor("out_0", (IMAGES, C, SIDE, SIDE), mybir.dt.float32, kind="ExternalOutput").ap())
    build(nc, *args)
    r = run_bass_kernel_spmd(nc, [arrays], core_ids=[0])
    return r.results[0]["out_0"]
```
